# Optimizing a Trainium2 kernel written in Bass

```python
import numpy as np
import jax
import jax.numpy as jnp

def _softmax(x, axis=-1):
    return jax.nn.softmax(x, axis=axis)

def _gelu(x):
    return jax.nn.gelu(x, approximate=True)

def _silu(x):
    return jax.nn.silu(x)

def _sigmoid(x):
    return jax.nn.sigmoid(x)

def _layernorm(x, axis=-1, eps=1e-05):
    m = jnp.mean(x, axis=axis, keepdims=True)
    v = jnp.var(x, axis=axis, keepdims=True)
    return (x - m) / jnp.sqrt(v + eps)

def _scatter_add(tgt, idx, src, axis=0):
    return tgt.at[idx].add(src)

def _segment_sum(src, seg, n):
    return jax.ops.segment_sum(src, seg, n)
kernel_name = 'mk_vit_tower_d2_tok_img768_r4_bd6747'

def setup_inputs(seed: int=0):
    np.random.seed(seed)
    _w = jnp.asarray

    def _rec_inputs():
        import jax
        import jax.numpy as jnp
        _rk = jax.random.key(seed)
        x = 7.57192e-06 + 1.00007 * jax.random.normal(jax.random.fold_in(_rk, 1), (16, 3, 96, 96), jnp.float32)
        return x
    x = _rec_inputs()

    def _L0_tok_setup():
        import jax, jax.numpy as jnp
        import numpy as np
        PATCH = 16
        HALF = PATCH // 2
        DIM = 192
        CH = 3
        PATCH_DIM = PATCH * PATCH * 5 * CH
        LN_EPS = 1e-05

        def _shift2d(x, t, l):
            H, W = (x.shape[-2], x.shape[-1])
            at, al = (abs(t), abs(l))
            xp = jnp.pad(x, ((0, 0), (0, 0), (at, at), (al, al)))
            return xp[:, :, at - t:at - t + H, al - l:al - l + W]
        key = jax.random.key(seed)
        k1, k2 = jax.random.split(key, 2)
        x = jax.random.normal(k1, (64, CH, 224, 224), dtype=jnp.float32)
        ln_gamma = jnp.ones((PATCH_DIM,), dtype=jnp.float32)
        ln_beta = jnp.zeros((PATCH_DIM,), dtype=jnp.float32)
        W = jax.random.normal(k2, (DIM, PATCH_DIM), dtype=jnp.float32) * np.float32(1.0 / np.sqrt(PATCH_DIM))
        b = jnp.zeros((DIM,), dtype=jnp.float32)
        return {'x': x, 'ln_gamma': ln_gamma, 'ln_beta': ln_beta, 'W': W, 'b': b}
    _L0_tok_all = _L0_tok_setup()
    _L0_tok_in = {k: v for k, v in _L0_tok_all.items() if k in ('ln_gamma', 'ln_beta', 'W', 'b')}
    del _L0_tok_all

    def _L0_attn_setup():
        import jax, jax.numpy as jnp
        import numpy as np
        LEVEL = 8
        NUM_HEADS = 12
        QN_SYM = float(-(LEVEL // 2))
        QP_SYM = float(LEVEL // 2 - 1)
        QN_ASYM = 0.0
        QP_ASYM = float(LEVEL - 1)

        def fake_quant(x, s, qn, qp):
            xc = jnp.clip(x / s, qn, qp)
            xr = xc + jax.lax.stop_gradient(jnp.round(xc) - xc)
            return s * xr
        key = jax.random.key(seed)
        k0, k1, k2 = jax.random.split(key, 3)
        B, N, C = (4, 512, 192)
        x = jax.random.normal(k0, (B, N, C), dtype=jnp.float32)
        Wqkv = jax.random.normal(k1, (3 * C, C), dtype=jnp.float32) * C ** (-0.5)
        Wproj = jax.random.normal(k2, (C, C), dtype=jnp.float32) * C ** (-0.5)
        bproj = jnp.zeros((C,), dtype=jnp.float32)
        s_q = jnp.asarray(1.0, dtype=jnp.float32)
        s_k = jnp.asarray(1.0, dtype=jnp.float32)
        s_v = jnp.asarray(1.0, dtype=jnp.float32)
        s_attn = jnp.asarray(1.0 / QP_ASYM, dtype=jnp.float32)
        s_after = jnp.asarray(1.0, dtype=jnp.float32)
        return {'x': x, 'Wqkv': Wqkv, 'Wproj': Wproj, 'bproj': bproj, 's_q': s_q, 's_k': s_k, 's_v': s_v, 's_attn': s_attn, 's_after': s_after}
    _L0_attn_all = _L0_attn_setup()
    _L0_attn_in = {k: v for k, v in _L0_attn_all.items() if k in ('Wqkv', 'Wproj', 'bproj', 's_q', 's_k', 's_v', 's_attn', 's_after')}
    del _L0_attn_all

    def _L0_ffn_setup():
        import jax, jax.numpy as jnp
        import numpy as np
        S, B, DIM = (256, 4, 192)
        N_EXPERTS = 8
        HID = 512
        key = jax.random.key(seed)
        ks = jax.random.split(key, 6)
        scale = 0.02
        return {'hidden_states': jax.random.normal(ks[0], (S, B, DIM), dtype=jnp.float32), 'router_w': jax.random.normal(ks[1], (DIM, N_EXPERTS), dtype=jnp.float32) * scale, 'router_b': jnp.zeros((N_EXPERTS,), dtype=jnp.float32), 'w1': jax.random.normal(ks[2], (N_EXPERTS, DIM, HID), dtype=jnp.float32) * scale, 'w2': jax.random.normal(ks[3], (N_EXPERTS, DIM, HID), dtype=jnp.float32) * scale, 'w3': jax.random.normal(ks[4], (N_EXPERTS, HID, DIM), dtype=jnp.float32) * scale}
    _L0_ffn_all = _L0_ffn_setup()
    _L0_ffn_in = {k: v for k, v in _L0_ffn_all.items() if k in ('router_w', 'router_b', 'w1', 'w2', 'w3')}
    del _L0_ffn_all

    def _L1_attn_setup():
        import jax, jax.numpy as jnp
        import numpy as np
        B_SZ, SEQ = (1, 512)
        D_MODEL, D_STATE, D_CONV, EXPAND = (192, 64, 4, 2)
        D_INNER = EXPAND * D_MODEL
        HEADDIM = 64
        NHEADS = D_INNER // HEADDIM
        CONV_DIM = D_INNER + 2 * D_STATE
        D_IN_PROJ = 2 * D_INNER + 2 * D_STATE + NHEADS
        HIDDEN = (D_MODEL * EXPAND + 127) // 128 * 128
        EPS = 1e-05

        def _ln(x, w, b):
            m = x.mean(-1, keepdims=True)
            v = ((x - m) ** 2).mean(-1, keepdims=True)
            return (x - m) * jax.lax.rsqrt(v + EPS) * w + b

        def _block(x, ln1_w, ln1_b, ln2_w, ln2_b, in_proj_w, conv_w, conv_b, dt_bias, A_log, D_skip, ssm_norm_w, out_proj_w, fc1_w, fc2_w):
            Bb, L, _ = x.shape
            h = _ln(x, ln1_w, ln1_b)
            zxbcdt = jnp.einsum('bld,pd->blp', h, in_proj_w)
            z = zxbcdt[..., :D_INNER]
            xBC = zxbcdt[..., D_INNER:D_INNER + CONV_DIM]
            dt = zxbcdt[..., D_INNER + CONV_DIM:]
            xp = jnp.pad(xBC, ((0, 0), (D_CONV - 1, 0), (0, 0)))
            xBC = sum((xp[:, k:k + L, :] * conv_w[:, k] for k in range(D_CONV))) + conv_b
            xBC = jax.nn.silu(xBC)
            xs = xBC[..., :D_INNER].reshape(Bb, L, NHEADS, HEADDIM)
            Bm = xBC[..., D_INNER:D_INNER + D_STATE]
            Cm = xBC[..., D_INNER + D_STATE:]
            dt = jax.nn.softplus(dt + dt_bias)
            dA = jnp.exp(dt * -jnp.exp(A_log))
            dtx = dt[..., None] * xs

            def step(hprev, inp):
                dA_t, dtx_t, B_t, C_t = inp
                hn = hprev * dA_t[:, :, None, None] + dtx_t[..., None] * B_t[:, None, None, :]
                return (hn, jnp.einsum('bhps,bs->bhp', hn, C_t))
            h0 = jnp.zeros((Bb, NHEADS, HEADDIM, D_STATE), x.dtype)
            _, ys = jax.lax.scan(step, h0, (dA.swapaxes(0, 1), dtx.swapaxes(0, 1), Bm.swapaxes(0, 1), Cm.swapaxes(0, 1)))
            y = ys.swapaxes(0, 1) + D_skip[None, None, :, None] * xs
            y = y.reshape(Bb, L, D_INNER) * jax.nn.silu(z)
            y = y * jax.lax.rsqrt((y * y).mean(-1, keepdims=True) + EPS) * ssm_norm_w
            x = x + jnp.einsum('bli,di->bld', y, out_proj_w)
            h2 = _ln(x, ln2_w, ln2_b)
            f = jnp.einsum('bld,hd->blh', h2, fc1_w)
            f = f[..., :HIDDEN] * jax.nn.silu(f[..., HIDDEN:])
            return x + jnp.einsum('blh,dh->bld', f, fc2_w)
        key = jax.random.key(seed)
        ks = jax.random.split(key, 8)
        s = 0.02
        return {'x': jax.random.normal(ks[0], (B_SZ, SEQ, D_MODEL), jnp.float32), 'ln1_w': jnp.ones((D_MODEL,), jnp.float32), 'ln1_b': jnp.zeros((D_MODEL,), jnp.float32), 'ln2_w': jnp.ones((D_MODEL,), jnp.float32), 'ln2_b': jnp.zeros((D_MODEL,), jnp.float32), 'in_proj_w': jax.random.normal(ks[1], (D_IN_PROJ, D_MODEL), jnp.float32) * s, 'conv_w': jax.random.normal(ks[2], (CONV_DIM, D_CONV), jnp.float32) * s, 'conv_b': jnp.zeros((CONV_DIM,), jnp.float32), 'dt_bias': jax.random.normal(ks[3], (NHEADS,), jnp.float32) * 0.1, 'A_log': jnp.log(jax.random.uniform(ks[4], (NHEADS,), jnp.float32, 1.0, 16.0)), 'D_skip': jnp.ones((NHEADS,), jnp.float32), 'ssm_norm_w': jnp.ones((D_INNER,), jnp.float32), 'out_proj_w': jax.random.normal(ks[5], (D_MODEL, D_INNER), jnp.float32) * s, 'fc1_w': jax.random.normal(ks[6], (2 * HIDDEN, D_MODEL), jnp.float32) * s, 'fc2_w': jax.random.normal(ks[7], (D_MODEL, HIDDEN), jnp.float32) * s}
    _L1_attn_all = _L1_attn_setup()
    _L1_attn_in = {k: v for k, v in _L1_attn_all.items() if k in ('ln1_w', 'ln1_b', 'ln2_w', 'ln2_b', 'in_proj_w', 'conv_w', 'conv_b', 'dt_bias', 'A_log', 'D_skip', 'ssm_norm_w', 'out_proj_w', 'fc1_w', 'fc2_w')}
    del _L1_attn_all

    def _L1_ffn_setup():
        import jax, jax.numpy as jnp
        import numpy as np
        B, T, D, E, K = (4, 512, 192, 8, 2)
        H = 4 * D
        key = jax.random.key(seed)
        k0, k1, k2, k3, k4 = jax.random.split(key, 5)
        s = 0.02
        return {'x': jax.random.normal(k0, (B, T, D), jnp.float32), 'router_w': jax.random.uniform(k1, (E, D), jnp.float32, -s * 0.1, s * 0.1), 'Wg': jax.random.uniform(k2, (E, H, D), jnp.float32, -s * 0.4, s * 0.4), 'Wu': jax.random.uniform(k3, (E, H, D), jnp.float32, -s * 0.4, s * 0.4), 'Wd': jax.random.normal(k4, (E, D, H), jnp.float32) * 0.01}
    _L1_ffn_all = _L1_ffn_setup()
    _L1_ffn_in = {k: v for k, v in _L1_ffn_all.items() if k in ('router_w', 'Wg', 'Wu', 'Wd')}
    del _L1_ffn_all
    return {'x': x, 'L0_tok_ln_gamma': _L0_tok_in['ln_gamma'], 'L0_tok_ln_beta': _L0_tok_in['ln_beta'], 'L0_tok_W': _L0_tok_in['W'], 'L0_tok_b': _L0_tok_in['b'], 'L0_attn_Wqkv': _L0_attn_in['Wqkv'], 'L0_attn_Wproj': _L0_attn_in['Wproj'], 'L0_attn_bproj': _L0_attn_in['bproj'], 'L0_attn_s_q': _L0_attn_in['s_q'], 'L0_attn_s_k': _L0_attn_in['s_k'], 'L0_attn_s_v': _L0_attn_in['s_v'], 'L0_attn_s_attn': _L0_attn_in['s_attn'], 'L0_attn_s_after': _L0_attn_in['s_after'], 'L0_ffn_router_w': _L0_ffn_in['router_w'], 'L0_ffn_router_b': _L0_ffn_in['router_b'], 'L0_ffn_w1': _L0_ffn_in['w1'], 'L0_ffn_w2': _L0_ffn_in['w2'], 'L0_ffn_w3': _L0_ffn_in['w3'], 'L1_attn_ln1_w': _L1_attn_in['ln1_w'], 'L1_attn_ln1_b': _L1_attn_in['ln1_b'], 'L1_attn_ln2_w': _L1_attn_in['ln2_w'], 'L1_attn_ln2_b': _L1_attn_in['ln2_b'], 'L1_attn_in_proj_w': _L1_attn_in['in_proj_w'], 'L1_attn_conv_w': _L1_attn_in['conv_w'], 'L1_attn_conv_b': _L1_attn_in['conv_b'], 'L1_attn_dt_bias': _L1_attn_in['dt_bias'], 'L1_attn_A_log': _L1_attn_in['A_log'], 'L1_attn_D_skip': _L1_attn_in['D_skip'], 'L1_attn_ssm_norm_w': _L1_attn_in['ssm_norm_w'], 'L1_attn_out_proj_w': _L1_attn_in['out_proj_w'], 'L1_attn_fc1_w': _L1_attn_in['fc1_w'], 'L1_attn_fc2_w': _L1_attn_in['fc2_w'], 'L1_ffn_router_w': _L1_ffn_in['router_w'], 'L1_ffn_Wg': _L1_ffn_in['Wg'], 'L1_ffn_Wu': _L1_ffn_in['Wu'], 'L1_ffn_Wd': _L1_ffn_in['Wd']}

def reference(x, L0_tok_ln_gamma, L0_tok_ln_beta, L0_tok_W, L0_tok_b, L0_attn_Wqkv, L0_attn_Wproj, L0_attn_bproj, L0_attn_s_q, L0_attn_s_k, L0_attn_s_v, L0_attn_s_attn, L0_attn_s_after, L0_ffn_router_w, L0_ffn_router_b, L0_ffn_w1, L0_ffn_w2, L0_ffn_w3, L1_attn_ln1_w, L1_attn_ln1_b, L1_attn_ln2_w, L1_attn_ln2_b, L1_attn_in_proj_w, L1_attn_conv_w, L1_attn_conv_b, L1_attn_dt_bias, L1_attn_A_log, L1_attn_D_skip, L1_attn_ssm_norm_w, L1_attn_out_proj_w, L1_attn_fc1_w, L1_attn_fc2_w, L1_ffn_router_w, L1_ffn_Wg, L1_ffn_Wu, L1_ffn_Wd):
    import jax
    import jax.numpy as jnp

    def _L0_tok_ref(x, ln_gamma, ln_beta, W, b):
        import jax, jax.numpy as jnp
        import numpy as np
        PATCH = 16
        HALF = PATCH // 2
        DIM = 192
        CH = 3
        PATCH_DIM = PATCH * PATCH * 5 * CH
        LN_EPS = 1e-05

        def _shift2d(x, t, l):
            H, W = (x.shape[-2], x.shape[-1])
            at, al = (abs(t), abs(l))
            xp = jnp.pad(x, ((0, 0), (0, 0), (at, at), (al, al)))
            return xp[:, :, at - t:at - t + H, al - l:al - l + W]
        p = PATCH
        shifts = ((1, -1, 1, -1), (-1, 1, -1, 1), (-1, 1, 1, -1), (1, -1, -1, 1))
        parts = [x] + [_shift2d(x, HALF * s[2], HALF * s[0]) for s in shifts]
        xc = jnp.concatenate(parts, axis=1)
        B, C5, H, Wd = xc.shape
        h, w = (H // p, Wd // p)
        patches = xc.reshape(B, C5, h, p, w, p)
        patches = patches.transpose(0, 2, 4, 3, 5, 1).reshape(B, h * w, p * p * C5)
        mu = patches.mean(axis=-1, keepdims=True)
        var = patches.var(axis=-1, keepdims=True)
        xn = (patches - mu) * jax.lax.rsqrt(var + LN_EPS) * ln_gamma + ln_beta
        return jnp.einsum('bnp,dp->bnd', xn, W) + b

    def _L0_attn_ref(x, Wqkv, Wproj, bproj, s_q, s_k, s_v, s_attn, s_after):
        import jax, jax.numpy as jnp
        import numpy as np
        LEVEL = 8
        NUM_HEADS = 12
        QN_SYM = float(-(LEVEL // 2))
        QP_SYM = float(LEVEL // 2 - 1)
        QN_ASYM = 0.0
        QP_ASYM = float(LEVEL - 1)

        def fake_quant(x, s, qn, qp):
            xc = jnp.clip(x / s, qn, qp)
            xr = xc + jax.lax.stop_gradient(jnp.round(xc) - xc)
            return s * xr
        B, N, C = x.shape
        H = NUM_HEADS
        D = C // H
        scale = D ** (-0.5)
        qkv = jnp.einsum('bnc,dc->bnd', x, Wqkv).reshape(B, N, 3, H, D).transpose(2, 0, 3, 1, 4)
        q, k, v = (qkv[0], qkv[1], qkv[2])
        q = fake_quant(q, s_q, QN_SYM, QP_SYM) * scale
        k = fake_quant(k, s_k, QN_SYM, QP_SYM)
        v = fake_quant(v, s_v, QN_SYM, QP_SYM)
        attn = jnp.einsum('bhnd,bhmd->bhnm', q, k)
        attn = fake_quant(attn / N, s_attn, QN_ASYM, QP_ASYM)
        out = jnp.einsum('bhnm,bhmd->bhnd', attn, v)
        out = fake_quant(out, s_after, QN_SYM, QP_SYM)
        out = out.transpose(0, 2, 1, 3).reshape(B, N, C)
        return out @ Wproj.T + bproj

    def _L0_ffn_ref(hidden_states, router_w, router_b, w1, w2, w3):
        import jax, jax.numpy as jnp
        import numpy as np
        S, B, DIM = (256, 4, 192)
        N_EXPERTS = 8
        HID = 512
        s, b, h = hidden_states.shape
        route = jax.nn.softmax(hidden_states @ router_w + router_b, axis=2)
        max_prob = jnp.max(route, axis=2).reshape(-1, 1)
        max_ind = jnp.argmax(route, axis=2).reshape(-1)
        x = hidden_states.reshape(-1, h)
        out = jnp.zeros_like(x)
        for e in range(N_EXPERTS):
            mask = (max_ind == e)[:, None]
            xe = jnp.where(mask, x, 0.0)
            oe = jax.nn.silu(xe @ w1[e]) * (xe @ w2[e]) @ w3[e]
            out = out + jnp.where(mask, oe, 0.0)
        out = out.astype(jnp.bfloat16) * max_prob
        return out.reshape(s, b, h)

    def _L1_attn_ref(x, ln1_w, ln1_b, ln2_w, ln2_b, in_proj_w, conv_w, conv_b, dt_bias, A_log, D_skip, ssm_norm_w, out_proj_w, fc1_w, fc2_w):
        import jax, jax.numpy as jnp
        import numpy as np
        B_SZ, SEQ = (1, 512)
        D_MODEL, D_STATE, D_CONV, EXPAND = (192, 64, 4, 2)
        D_INNER = EXPAND * D_MODEL
        HEADDIM = 64
        NHEADS = D_INNER // HEADDIM
        CONV_DIM = D_INNER + 2 * D_STATE
        D_IN_PROJ = 2 * D_INNER + 2 * D_STATE + NHEADS
        HIDDEN = (D_MODEL * EXPAND + 127) // 128 * 128
        EPS = 1e-05

        def _ln(x, w, b):
            m = x.mean(-1, keepdims=True)
            v = ((x - m) ** 2).mean(-1, keepdims=True)
            return (x - m) * jax.lax.rsqrt(v + EPS) * w + b

        def _block(x, ln1_w, ln1_b, ln2_w, ln2_b, in_proj_w, conv_w, conv_b, dt_bias, A_log, D_skip, ssm_norm_w, out_proj_w, fc1_w, fc2_w):
            Bb, L, _ = x.shape
            h = _ln(x, ln1_w, ln1_b)
            zxbcdt = jnp.einsum('bld,pd->blp', h, in_proj_w)
            z = zxbcdt[..., :D_INNER]
            xBC = zxbcdt[..., D_INNER:D_INNER + CONV_DIM]
            dt = zxbcdt[..., D_INNER + CONV_DIM:]
            xp = jnp.pad(xBC, ((0, 0), (D_CONV - 1, 0), (0, 0)))
            xBC = sum((xp[:, k:k + L, :] * conv_w[:, k] for k in range(D_CONV))) + conv_b
            xBC = jax.nn.silu(xBC)
            xs = xBC[..., :D_INNER].reshape(Bb, L, NHEADS, HEADDIM)
            Bm = xBC[..., D_INNER:D_INNER + D_STATE]
            Cm = xBC[..., D_INNER + D_STATE:]
            dt = jax.nn.softplus(dt + dt_bias)
            dA = jnp.exp(dt * -jnp.exp(A_log))
            dtx = dt[..., None] * xs

            def step(hprev, inp):
                dA_t, dtx_t, B_t, C_t = inp
                hn = hprev * dA_t[:, :, None, None] + dtx_t[..., None] * B_t[:, None, None, :]
                return (hn, jnp.einsum('bhps,bs->bhp', hn, C_t))
            h0 = jnp.zeros((Bb, NHEADS, HEADDIM, D_STATE), x.dtype)
            _, ys = jax.lax.scan(step, h0, (dA.swapaxes(0, 1), dtx.swapaxes(0, 1), Bm.swapaxes(0, 1), Cm.swapaxes(0, 1)))
            y = ys.swapaxes(0, 1) + D_skip[None, None, :, None] * xs
            y = y.reshape(Bb, L, D_INNER) * jax.nn.silu(z)
            y = y * jax.lax.rsqrt((y * y).mean(-1, keepdims=True) + EPS) * ssm_norm_w
            x = x + jnp.einsum('bli,di->bld', y, out_proj_w)
            h2 = _ln(x, ln2_w, ln2_b)
            f = jnp.einsum('bld,hd->blh', h2, fc1_w)
            f = f[..., :HIDDEN] * jax.nn.silu(f[..., HIDDEN:])
            return x + jnp.einsum('blh,dh->bld', f, fc2_w)
        return _block(x, ln1_w, ln1_b, ln2_w, ln2_b, in_proj_w, conv_w, conv_b, dt_bias, A_log, D_skip, ssm_norm_w, out_proj_w, fc1_w, fc2_w)

    def _L1_ffn_ref(x, router_w, Wg, Wu, Wd):
        import jax, jax.numpy as jnp
        import numpy as np
        B, T, D, E, K = (4, 512, 192, 8, 2)
        H = 4 * D
        Bv, Tv, Dv = x.shape
        N = Bv * Tv
        xf = x.reshape(N, Dv)
        logits = (xf @ router_w.T).astype(jnp.float32)
        top_logits, top_idx = jax.lax.top_k(logits, K)
        top_w = jax.nn.softmax(top_logits, axis=-1).astype(x.dtype)
        out = jnp.zeros_like(xf)
        for e in range(E):
            w_e = jnp.sum(top_w * (top_idx == e), axis=-1)
            h = jax.nn.silu(xf @ Wg[e].T) * (xf @ Wu[e].T)
            out = out + h @ Wd[e].T * w_e[:, None]
        return out.reshape(Bv, Tv, Dv)
    h = _L0_tok_ref(x, L0_tok_ln_gamma, L0_tok_ln_beta, L0_tok_W, L0_tok_b)
    h = h + _L0_attn_ref(_layernorm(h, axis=-1), L0_attn_Wqkv, L0_attn_Wproj, L0_attn_bproj, L0_attn_s_q, L0_attn_s_k, L0_attn_s_v, L0_attn_s_attn, L0_attn_s_after)
    h = h + _L0_ffn_ref(_layernorm(h, axis=-1), L0_ffn_router_w, L0_ffn_router_b, L0_ffn_w1, L0_ffn_w2, L0_ffn_w3)
    h = h + _L1_attn_ref(_layernorm(h, axis=-1), L1_attn_ln1_w, L1_attn_ln1_b, L1_attn_ln2_w, L1_attn_ln2_b, L1_attn_in_proj_w, L1_attn_conv_w, L1_attn_conv_b, L1_attn_dt_bias, L1_attn_A_log, L1_attn_D_skip, L1_attn_ssm_norm_w, L1_attn_out_proj_w, L1_attn_fc1_w, L1_attn_fc2_w)
    h = h + _L1_ffn_ref(_layernorm(h, axis=-1), L1_ffn_router_w, L1_ffn_Wg, L1_ffn_Wu, L1_ffn_Wd)
    return h

_drawn_inputs = setup_inputs


def setup_inputs(seed=0):
    import zlib

    import numpy as np

    out = dict(_drawn_inputs(seed))
    spreads = {'L0_tok_ln_gamma': (1.0, 0.2),
     'L0_tok_ln_beta': (0.0, 0.1),
     'L0_tok_b': (0.0, 0.1),
     'L0_attn_bproj': (0.0, 0.1),
     'L0_ffn_router_b': (0.0, 0.8),
     'L1_attn_ln1_w': (1.0, 0.2),
     'L1_attn_ln1_b': (0.0, 0.49),
     'L1_attn_ln2_w': (1.0, 0.6),
     'L1_attn_ln2_b': (0.0, 0.8),
     'L1_attn_conv_b': (0.0, 0.1),
     'L1_attn_D_skip': (1.0, 0.2),
     'L1_attn_ssm_norm_w': (1.0, 0.2)}
    factors = {'L0_ffn_router_w': 8.0,
     'L0_ffn_w1': 8.0,
     'L0_ffn_w2': 8.0,
     'L0_ffn_w3': 8.0,
     'L1_attn_conv_w': 2.758,
     'L1_attn_dt_bias': 54.76,
     'L1_attn_A_log': 64.0,
     'L1_attn_fc1_w': 6.981,
     'L1_attn_fc2_w': 6.939,
     'L1_ffn_router_w': 47.753,
     'L1_ffn_Wg': 43.237,
     'L1_ffn_Wu': 41.876,
     'L1_ffn_Wd': 42.125}
    for name, (base, spread) in spreads.items():
        noise = np.random.default_rng([zlib.crc32(name.encode()), seed]).standard_normal(out[name].shape)
        drawn = base * np.exp(spread * noise) if base else spread * noise
        out[name] = jnp.asarray(drawn.astype(out[name].dtype))
    for name, factor in factors.items():
        out[name] = (out[name] * factor).astype(out[name].dtype)
    return out
```

```python
from contextlib import ExitStack

import numpy as np
import concourse.bass as bass
from concourse import mybir

ALU = mybir.AluOpType
ACT = mybir.ActivationFunctionType
F32 = mybir.dt.float32
BF16 = mybir.dt.bfloat16
I32 = mybir.dt.int32
U32 = mybir.dt.uint32
AX = mybir.AxisListType

P = 128
IMGS, CH, SIDE, PATCH = 16, 3, 96, 16
GRID = SIDE // PATCH
NTOK = GRID * GRID
T = IMGS * NTOK
TT = (T + P - 1) // P
TPAD = TT * P
LAST = T - (TT - 1) * P
D, DH, DM = 192, 96, 2
HB = IMGS // 2 * NTOK
WIN = GRID + 1
NWIN = IMGS * WIN * WIN
NCH = CH * 2 * 4
NALL = NCH + CH * 2
KTOK = PATCH * PATCH * CH * 5
PAIRS = IMGS // 2
HEADS, HD = 12, 16
HH = HEADS // 2
QLO, QHI, AHI = -4.0, 3.0, 7.0
MAGIC = 12582912.0
EPS = 1e-5
E = 8
SSH, SSD, SSN = 6, 64, 64
DI = SSH * SSD
DC = 4
HP = DI // P
SEG = NTOK + DC - 1
M1_TILES = (T + E * (P - 1)) // P
M2_TILES = (2 * T + E * (P - 1)) // P
M1_H, M2_H = 512, 768
SUMS = 8
N_CONST = 25
W2 = 2 * HH * NTOK
SEGW = SSH * NTOK


def token_sums(eng, first, src, row, tot, step):
    w = src.rearrange("p y (r x) -> p (y r) x", x=WIN)
    step(eng.tensor_tensor(row.rearrange("p y r x -> p (y r) x"), w[:, :, 0:GRID], w[:, :, 1:WIN], ALU.add))
    r = row.rearrange("p y (b r) x -> p y b (r x)", r=WIN)
    t = tot[:, 0:T].rearrange("p (b n) -> p b n", n=NTOK)
    step(eng.tensor_tensor(t, r[:, 0, :, 0:NTOK], r[:, 0, :, GRID:GRID + NTOK], ALU.add))
    step(eng.tensor_tensor(t, t, r[:, 1, :, 0:NTOK], ALU.add))
    step(eng.tensor_tensor(t, t, r[:, 1, :, GRID:GRID + NTOK], ALU.add))
    for wy in range(2):
        for xh in range(2):
            half = slice(64 * xh, 64 * xh + 64)
            c = src[half, 1 - wy].rearrange("p (b r x) -> p b r x", r=WIN, x=WIN)
            c = c[:, :, wy:wy + GRID, 1 - xh:1 - xh + GRID]
            th = tot[half, 0:T].rearrange("p (b r x) -> p b r x", r=GRID, x=GRID)
            step(eng.tensor_tensor(th, th, c, ALU.add))


def build(nc, A, out):
    with ExitStack() as ctx:
        def sb(name, shape, dt=F32, scope=ctx):
            return scope.enter_context(nc.sbuf_tensor(name, shape, dt))

        ps = ctx.enter_context(nc.psum_tensor("ps", [P, 8, 512], F32))

        def row_of(b, n, parts=P):
            return ps[0:parts, b:b + n, :].rearrange("p b n -> p (b n)")

        def two_halves(b, parts=P):
            return ps[0:parts, b:b + 2, 0:HB]

        def scratch(name, n, dt):
            return nc.dram_tensor(name, (n * P, D), dt, kind="Internal").ap()

        sorted_x = [scratch("sorted_x0", M1_TILES, F32), scratch("sorted_x1", M2_TILES, F32)]
        sorted_y = [scratch("sorted_y0", M1_TILES, BF16), scratch("sorted_y1", M2_TILES, F32)]

        ident = sb("ident", [P, P])
        identb = sb("identb", [P, P], BF16)
        ones = sb("ones", [P, P])
        onesb = sb("onesb", [P, P], BF16)
        earlier = sb("earlier", [P, P], BF16)
        head_mask = sb("head_mask", [DH, HH])
        later_blk = sb("later_blk", [P, P])
        upto = sb("upto", [P, NTOK])
        causal = sb("causal", [P, 2, NTOK])
        iota_e = sb("iota_e", [P, E])
        iota_t = sb("iota_t", [1, M2_TILES, E])
        inv_k = sb("inv_k", [P, 1])
        eps_t = sb("eps_t", [P, 1])
        magic_t = sb("magic_t", [P, 1])
        zeros = sb("zeros", [P, D])
        ones8 = sb("ones8", [P, E])

        wqkv = sb("wqkv", [DH, DM, 3 * D])
        wproj = sb("wproj", [DH, DM, D])
        bproj = sb("bproj", [P, D])
        scales = sb("scales", [P, 5])
        tok_b = sb("tok_b", [1, D])
        rw = [sb("rw1", [DH, DM, E]), sb("rw2", [DH, DM, E])]
        rb1 = sb("rb1", [P, E])
        inproj = sb("inproj", [DH, DM, 2 * DI + 2 * SSN + SSH])
        convw = sb("convw", [P, HP + 1, DC])
        convb = sb("convb", [P, HP + 1])
        dskip = sb("dskip", [P, HP])
        dtb = sb("dtb", [P, SSH])
        alog = sb("alog", [P, SSH])
        normw = sb("normw", [P, HP])
        outproj = sb("outproj", [P, HP, D])
        fc1 = sb("fc1", [DH, DM, 2 * DI])
        fc2 = sb("fc2", [P, HP, D])
        ln1 = sb("ln1", [DH, 2, DM])
        ln2 = sb("ln2", [DH, 2, DM])
        w12 = [sb(f"w12_{i}", [DH, DM, 2 * M2_H]) for i in range(2)]
        w3 = [sb(f"w3_{i}", [P, M2_H // P, D]) for i in range(2)]

        h = sb("h", [P, TT, D])
        hb = sb("hb", [P, TT, D])
        xn = sb("xn", [P, TT, D])
        xt = sb("xt", [DH, DM, TPAD])
        xtp = sb("xtp", [DH, DM, IMGS, 64])
        st6 = sb("st6", [P, TT, 6])
        mv = sb("mv", [P, TT, 2])
        std = sb("std", [P, TT])
        rstd = sb("rstd", [P, TT])
        var2 = sb("var2", [P, TT])
        rstd2 = sb("rstd2", [P, TT])

        logit = sb("logit", [P, TT, E])
        below = sb("below", [P, TT, E])
        ex8 = sb("ex8", [P, TT, E])
        top8 = sb("top8", [P, TT, 8])
        idx8 = sb("idx8", [P, TT, 8], U32)
        idxf = sb("idxf", [P, TT, 2])
        oh = sb("oh", [P, 2, TT, E])
        ohb = sb("ohb", [P, TT, E], BF16)
        tiles_e = sb("tiles_e", [P, E])
        cum_e = sb("cum_e", [P, E])
        base_e = sb("base_e", [P, E])
        rank_b = sb("rank_b", [P, TT, E])
        pick = sb("pick", [P, 2, TT, E])
        slotf = sb("slotf", [P, 2, TT])
        slot = sb("slot", [P, 2, TT], I32)
        teb = sb("teb", [1, M2_TILES, E])
        tef = sb("tef", [1, M2_TILES])
        te = sb("te", [1, M2_TILES], I32)
        gsum = sb("gsum", [P, TT])
        gate = sb("gate", [P, 2, TT])

        arena = ExitStack()
        xw = sb("xw", [P, CH, 2, NWIN], scope=arena)
        xsq = sb("xsq", [P, CH, 2, NWIN], scope=arena)
        xsum = sb("xsum", [P, 2, NWIN], scope=arena)
        wall = sb("wall", [P, NALL, D], scope=arena)
        weff = sb("weff", [P, NCH, D], scope=arena)
        wug = sb("wug", [P, CH * 2, D], scope=arena)
        gam = sb("gam", [P, NALL], scope=arena)
        bet = sb("bet", [P, NALL], scope=arena)
        row = sb("row", [P, 2, 2, IMGS * WIN, GRID], scope=arena)
        tot = sb("tot", [P, 2, TPAD], scope=arena)
        acc = sb("acc", [P, 2, D], scope=arena)
        s12 = sb("s12", [P, 2, D], scope=arena)
        mom = sb("mom", [P, TT, 2], scope=arena)
        negmu = sb("negmu", [P, TT], scope=arena)
        var = sb("var", [P, TT], scope=arena)
        arena.close()

        arena = ExitStack()
        qf = sb("qf", [DH, 4, T], scope=arena)
        qi = sb("qi", [DH, DM, T], scope=arena)
        kc = sb("kc", [DH, DM, T], scope=arena)
        ki = sb("ki", [DH, DM, IMGS, 64], BF16, scope=arena)
        qe = sb("qe", [DH, DM, IMGS, HH, NTOK], BF16, scope=arena)
        vf = sb("vf", [P, PAIRS, D], scope=arena)
        vc = sb("vc", [P, PAIRS, D], scope=arena)
        vi = sb("vi", [P, 2, PAIRS, D], BF16, scope=arena)
        pre = sb("pre", [P, 2, W2], scope=arena)
        rnd = sb("rnd", [P, 2, W2], scope=arena)
        at = sb("at", [P, 2, 512], BF16, scope=arena)
        of = sb("of", [P, PAIRS, D], scope=arena)
        oc = sb("oc", [P, PAIRS, D], scope=arena)
        oi = sb("oi", [P, PAIRS, D], BF16, scope=arena)
        ot = sb("ot", [DH, DM, TPAD], scope=arena)
        rsc = sb("rsc", [P, 5], scope=arena)
        c_sc = sb("c_sc", [P, 4], scope=arena)
        arena.close()

        arena = ExitStack()
        xg = sb("xg", [P, M2_TILES, D], scope=arena)
        xgt = sb("xgt", [DH, DM, M2_TILES * P], scope=arena)
        sg = sb("sg", [P, 2, M2_H // 2], scope=arena)
        ht = sb("ht", [P, 2, M2_H // 2], scope=arena)
        ysb = [sb("ysb0", [P, 2, D], BF16, scope=arena), sb("ysb1", [P, 2, D], scope=arena)]
        yg = [sb("yg0", [P, 1, TT, D], BF16, scope=arena), sb("yg1", [P, 2, TT, D], scope=arena)]
        arena.close()

        arena = ExitStack()
        xn2 = sb("xn2", [P, TT, D], scope=arena)
        xpad = sb("xpad", [P, HP + 1, IMGS, SEG], scope=arena)
        cv = sb("cv", [P, HP + 1, IMGS, NTOK], scope=arena)
        xst = sb("xst", [P, HP, IMGS, 64], scope=arena)
        bt = sb("bt", [SSN, IMGS, 64], scope=arena)
        ct = sb("ct", [SSN, IMGS, 64], scope=arena)
        zs = sb("zs", [P, HP, T], scope=arena)
        dtw = sb("dtw", [P, 8, PAIRS, SSH], scope=arena)
        nega = sb("nega", [P, 3, SSH], scope=arena)
        av = sb("av", [P, PAIRS, SSH, NTOK], scope=arena)
        dec = sb("dec", [P, PAIRS, SSH, NTOK], scope=arena)
        gm = sb("gm", [P, PAIRS, 2, NTOK], scope=arena)
        mix = sb("mix", [P, PAIRS, SSH, 2, NTOK], scope=arena)
        dtx = sb("dtx", [P, PAIRS, DI], scope=arena)
        yt = sb("yt", [P, HP, TPAD], scope=arena)
        ysq = sb("ysq", [P, HP, TPAD], scope=arena)
        x2 = sb("x2", [P, TT, D], scope=arena)
        arena.close()
        ft, sgf = yt, ysq

        S = {n: ctx.enter_context(nc.semaphore(n)) for n in """
            d_gam d_x0 d_x1 d_x2 d_w0 d_w1 d_w2 d_wu d_att d_ssm d_zero1 d_zero2 d_out
            d_scat1 d_scat2 d_xg0 d_xg1 d_xg2 d_xg3 d_w12a d_w12b d_w3a d_w3b d_ya d_yb d_yg
            g_const g_pad g_sq g_beta g_wout g_hb g_at g_ssm
            v_c v_wug v_weff v_st v_acc v_hd v_h v_bn v_mv v_xn v_xt v_qe v_ki v_vi v_pre v_clip v_oi v_ot
            v_var v_v2 v_lg v_oh v_slot v_te v_gt v_ht v_cv v_u v_one v_av v_gm v_mix v_dtx v_ys v_yz
            v_x2 v_fc v_cs
            a_sq a_hd a_s12 a_std a_xt a_qf a_vf a_rnd a_of a_ot a_ex a_gt a_sg a_y a_cp a_z a_xs a_dt
            a_dec a_ysq a_fc
            p_tok p_st p_ht p_tr p_qk p_v p_sc p_av p_otr p_proj p_lg p_rk p_gt p_gu p_y p_in p_dt p_g
            p_seg p_xs p_ys p_ssq p_out p_fc p_f2""".split()}
        d_w12 = (S["d_w12a"], S["d_w12b"])
        d_w3 = (S["d_w3a"], S["d_w3b"])
        d_y = (S["d_ya"], S["d_yb"])
        MOE = (dict(n=M1_TILES, hid=M1_H, k=1, w12=A["m1_w12"], w3=A["m1_w3"], before=0),
               dict(n=M2_TILES, hid=M2_H, k=2, w12=A["m2_w12"], w3=A["m2_w3"], before=M1_TILES))
        N_ATT, N_SSM, N_FIRST = 16 * 7, 16 * 13, 7

        block = ctx.enter_context(nc.Block())

        @block.sync
        def _(sp):
            def load(dst, src, s):
                sp.dma_start(dst, src).then_inc(S[s], 16)

            load(gam[:], A["gam"], "d_gam")
            load(bet[:], A["bet"], "d_gam")
            load(wall[:, NCH:NALL, :], A["w_un"], "d_wu")
            for c in range(CH):
                load(wall[:, 8 * c:8 * c + 8, :], A["w_sh"][:, 8 * c:8 * c + 8, :], f"d_w{c}")
                load(xw[:, c], A["xw"][:, c], f"d_x{c}")
            for dst, name in ((wqkv, "wqkv"), (wproj, "wproj"), (bproj, "bproj"), (scales, "scales"),
                              (tok_b, "tok_b"), (rw[0], "rw1"), (rb1, "rb1")):
                load(dst[:], A[name], "d_att")
            for dst, name in ((rw[1], "rw2"), (inproj, "inproj"), (convw, "convw"), (convb, "convb"),
                              (dskip, "dskip"), (dtb, "dtb"), (alog, "alog"), (normw, "normw"),
                              (outproj, "outproj"), (fc1, "fc1"), (fc2, "fc2"), (ln1, "ln1"), (ln2, "ln2")):
                load(dst[:], A[name], "d_ssm")
            sp.wait_ge(S["g_const"], 1)
            for m in range(2):
                load(sorted_x[m].rearrange("(n p) d -> p n d", p=P),
                     zeros[:].unsqueeze(1).broadcast_to([P, MOE[m]["n"], D]), f"d_zero{m + 1}")

            def experts_io(m):
                r = MOE[m]
                n, hid, before = r["n"], r["hid"], r["before"]

                def expert(j):
                    return sp.value_load(te[0:1, bass.ds(j, 1)], min_val=0, max_val=E - 1)

                def up_weights(e, b):
                    sp.dma_start(w12[b][:, :, 0:2 * hid],
                                 r["w12"][bass.ds(e, 1)].rearrange("e p m n -> (e p) m n")).then_inc(d_w12[b], 16)

                def down_weights(e, b):
                    sp.dma_start(w3[b][:, 0:hid // P, :],
                                 r["w3"][bass.ds(e, 1)].rearrange("e p c n -> (e p) c n")).then_inc(d_w3[b], 16)

                sp.wait_ge(S["v_te"], m + 1)
                for b in range(2):
                    e = expert(b)
                    up_weights(e, b)
                    down_weights(e, b)
                sp.wait_ge(S[f"d_scat{m + 1}"], 16 * TT * r["k"])
                q = n // 4
                for i in range(4):
                    load(xg[:, q * i:q * i + q, :],
                         sorted_x[m].rearrange("(n p) d -> p n d", p=P)[:, q * i:q * i + q, :], f"d_xg{i}")
                with sp.Fori(1, n // 2) as i:
                    for b in range(2):
                        e = expert(i * 2 + b)
                        sp.wait_ge(S["p_gu"], i * 4 + (2 * b - 2 + 2 * before))
                        up_weights(e, b)
                        sp.wait_ge(S["p_y"], i * 2 + (b - 1 + before))
                        down_weights(e, b)

            experts_io(0)
            experts_io(1)
            for t in range(TT):
                rows = P if t < TT - 1 else LAST
                sp.wait_ge(S["v_h"], 4 * TT + 2 * t + 2)
                load(out[t * P:t * P + rows, :], h[0:rows, t, :], "d_out")
            sp.wait_ge(S["d_out"], 16 * TT)

        @block.gpsimd
        def _(pool):
            g = nc.gpsimd
            made = [0]

            def const(ins):
                made[0] += 1
                ins.then_inc(S["g_const"], 1)
                pool.wait_ge(S["g_const"], made[0])

            const(g.memset(zeros[:], 0.0))
            const(g.memset(ones[:], 1.0))
            const(g.memset(inv_k[:], 1.0 / KTOK))
            const(g.memset(eps_t[:], EPS))
            const(g.memset(magic_t[:], MAGIC))
            const(g.memset(tot[:, :, T:TPAD], 0.0))
            const(g.affine_select(out=ident[:], in_=ones[:], compare_op=ALU.is_equal, fill=0.0, base=0,
                                  pattern=[[-1, P]], channel_multiplier=1))
            assert made[0] == N_FIRST
            g.memset(xt[:, :, T:TPAD], 0.0).then_inc(S["g_pad"], 1)
            g.memset(xtp[:, :, :, NTOK:64], 0.0).then_inc(S["g_pad"], 1)

            n_sq = [0]

            def step(ins):
                n_sq[0] += 1
                ins.then_inc(S["g_sq"], 1)
                pool.wait_ge(S["g_sq"], n_sq[0])

            pool.wait_ge(S["a_sq"], 2)
            step(g.tensor_tensor(xsq[:, 0], xsq[:, 0], xsq[:, 1], ALU.add))
            pool.wait_ge(S["a_sq"], 3)
            step(g.tensor_tensor(xsq[:, 0], xsq[:, 0], xsq[:, 2], ALU.add))
            token_sums(g, 0, xsq[:, 0], row[:, 1], tot[:, 1], step)
            assert n_sq[0] == SUMS + 2
            pool.wait_ge(S["v_weff"], 3 * CH)
            pool.wait_ge(S["v_wug"], 1)
            pool.wait_ge(S["d_gam"], 32)
            g.tensor_tensor(wall[:], wall[:], bet[:].unsqueeze(2).broadcast_to([P, NALL, D]),
                            ALU.mult).then_inc(S["g_beta"], 1)

            const(g.memset(onesb[:], 1.0))
            const(g.memset(ones8[:], 1.0))
            const(g.memset(later_blk[:], 0.0))
            const(g.memset(causal[:], 0.0))
            const(g.affine_select(out=identb[:], in_=ones[:], compare_op=ALU.is_equal, fill=0.0, base=0,
                                  pattern=[[-1, P]], channel_multiplier=1))
            const(g.affine_select(out=earlier[:], in_=ones[:], compare_op=ALU.is_gt, fill=0.0, base=0,
                                  pattern=[[1, P]], channel_multiplier=-1))
            const(g.affine_select(out=head_mask[:], in_=ones[0:DH, 0:HH], compare_op=ALU.is_ge, fill=0.0,
                                  base=0, pattern=[[-HD, HH]], channel_multiplier=1))
            const(g.affine_select(out=head_mask[:], in_=head_mask[:], compare_op=ALU.is_ge, fill=0.0,
                                  base=HD - 1, pattern=[[HD, HH]], channel_multiplier=-1))
            for i in range(2):
                r = slice(64 * i, 64 * i + 64)
                const(g.affine_select(out=later_blk[r, r], in_=ones[r, 0:64], compare_op=ALU.is_gt, fill=0.0,
                                      base=0, pattern=[[-1, 64]], channel_multiplier=1))
                const(g.affine_select(out=later_blk[r, r], in_=later_blk[r, r], compare_op=ALU.is_ge, fill=0.0,
                                      base=NTOK - 1, pattern=[[0, 64]], channel_multiplier=-1))
                const(g.affine_select(out=upto[r, :], in_=ones[r, 0:NTOK], compare_op=ALU.is_ge, fill=0.0,
                                      base=0, pattern=[[1, NTOK]], channel_multiplier=-1))
                const(g.affine_select(out=causal[r, i, :], in_=ones[r, 0:NTOK], compare_op=ALU.is_ge, fill=0.0,
                                      base=0, pattern=[[1, NTOK]], channel_multiplier=-1))
            const(g.iota(iota_e[:], pattern=[[1, E]], base=0, channel_multiplier=0,
                         allow_small_or_imprecise_dtypes=True))
            const(g.iota(iota_t[:], pattern=[[1, M2_TILES], [0, E]], base=0, channel_multiplier=0,
                         allow_small_or_imprecise_dtypes=True))
            assert made[0] == N_CONST

            pool.wait_ge(S["v_h"], TT)
            g.memset(ki[:, :, :, NTOK:64], 0.0).then_inc(S["g_pad"], 1)
            g.memset(vi[:], 0.0).then_inc(S["g_pad"], 1)
            g.memset(at[:, :, W2:512], 0.0).then_inc(S["g_pad"], 1)
            g.memset(ot[:, :, T:TPAD], 0.0).then_inc(S["g_pad"], 1)
            pool.wait_ge(S["d_att"], N_ATT)
            g.tensor_tensor(hb[:], h[:], bproj[:].unsqueeze(1).broadcast_to([P, TT, D]), ALU.add)\
                .then_inc(S["g_hb"], 1)
            pool.wait_ge(S["d_ssm"], N_SSM)
            g.tensor_tensor(outproj[:], outproj[:], normw[:].unsqueeze(2).broadcast_to([P, HP, D]), ALU.mult)\
                .then_inc(S["g_wout"], 1)
            pool.wait_ge(S["g_pad"], 6)
            for j in range(PAIRS):
                pool.wait_ge(S["a_rnd"], j + 1)
                if j >= 2:
                    pool.wait_ge(S["p_av"], j - 1)
                g.tensor_scalar(at[:, j % 2, 0:W2], rnd[:, j % 2, :], MAGIC, None, ALU.subtract)\
                    .then_inc(S["g_at"], 1)

            def experts_io(m):
                r = MOE[m]
                n, before = r["n"], r["before"]
                pool.wait_ge(S["v_slot"], m + 1)
                pool.wait_ge(S["v_xn"], TT * (2 if m == 0 else 6))
                pool.wait_ge(S[f"d_zero{m + 1}"], 16)
                for k in range(r["k"]):
                    for t in range(TT):
                        rows = P if t < TT - 1 else LAST
                        g.indirect_dma_start(
                            sorted_x[m], bass.IndirectOffsetOnAxis(ap=slot[0:rows, k, t:t + 1], axis=0),
                            xn[0:rows, t, :], None).then_inc(S[f"d_scat{m + 1}"], 16)
                with pool.Fori(0, n // 2) as i:
                    for b in range(2):
                        pool.wait_ge(S["a_y"], i * 2 + (b + 1 + before))
                        dst = sorted_y[m].rearrange("(n p) d -> n p d", p=P)[bass.ds(i * 2 + b, 1)]
                        g.dma_start(dst.rearrange("n p d -> (n p) d"), ysb[m][:, b, :]).then_inc(d_y[b], 16)
                for b in range(2):
                    pool.wait_ge(d_y[b], 8 * (n + before))
                for t in range(TT):
                    for k in range(r["k"]):
                        rows = P if t < TT - 1 else LAST
                        g.indirect_dma_start(
                            yg[m][0:rows, k, t, :], None, sorted_y[m],
                            bass.IndirectOffsetOnAxis(ap=slot[0:rows, k, t:t + 1], axis=0))\
                            .then_inc(S["d_yg"], 16)

            experts_io(0)
            pool.wait_ge(S["v_h"], 3 * TT)
            g.memset(xpad[:, :, :, 0:DC - 1], 0.0).then_inc(S["g_ssm"], 1)
            g.memset(xst[:, :, :, NTOK:64], 0.0).then_inc(S["g_ssm"], 1)
            g.memset(bt[:, :, NTOK:64], 0.0).then_inc(S["g_ssm"], 1)
            g.memset(yt[:, :, T:TPAD], 0.0).then_inc(S["g_ssm"], 1)
            g.memset(ysq[:, :, T:TPAD], 0.0).then_inc(S["g_ssm"], 1)
            pool.wait_ge(S["v_x2"], TT)
            g.tensor_tensor(hb[:], h[:], x2[:], ALU.add).then_inc(S["g_hb"], 1)
            experts_io(1)

        @block.scalar
        def _(act):
            a = nc.scalar
            for c in range(CH):
                act.wait_ge(S[f"d_x{c}"], 16)
                a.activation(xsq[:, c], xw[:, c], ACT.Square).then_inc(S["a_sq"], 1)
            act.wait_ge(S["p_tok"], 2)
            a.copy(xt[:, 0, 0:T].rearrange("p (b n) -> p b n", b=2), two_halves(0, DH)).then_inc(S["a_hd"], 1)
            act.wait_ge(S["p_st"], 3)
            a.copy(s12[:].rearrange("p s d -> p (s d)"), ps[:, 5, 0:2 * D]).then_inc(S["a_s12"], 1)
            act.wait_ge(S["v_var"], 1)
            a.activation(std[:], var[:], ACT.Sqrt, bias=eps_t[:]).then_inc(S["a_std"], 1)

            def deviations(i):
                act.wait_ge(S["v_mv"], TT * i)
                a.activation(std[:], mv[:, :, 1], ACT.Sqrt, bias=eps_t[:]).then_inc(S["a_std"], 1)

            def transposed(i, padded=False, ln=None):
                act.wait_ge(S["p_tr"], 2 * i - 1)
                act.wait_ge(S["g_pad"], 2)
                src = row_of(0, 2, DH)[:, 0:T]
                dst = xt[:, 0, 0:T]
                if padded:
                    src = src.rearrange("p (b n) -> p b n", n=NTOK)
                    dst = xtp[:, 0, :, 0:NTOK]
                if ln is None:
                    a.copy(dst, src).then_inc(S["a_xt"], 1)
                else:
                    act.wait_ge(S["d_ssm"], N_SSM)
                    a.activation(dst, src, ACT.Identity, bias=ln[:, 1, 0:1],
                                 scale=ln[:, 0, 0:1]).then_inc(S["a_xt"], 1)

            deviations(1)
            transposed(1, padded=True)
            act.wait_ge(S["v_cs"], 3)
            for r in range(4):
                act.wait_ge(S["p_qk"], r + 1)
                a.activation(qf[:, r, :].rearrange("p (b n) -> p b n", b=2), two_halves(2 * r, DH), ACT.Identity,
                             bias=magic_t[0:DH, :], scale=rsc[0:DH, r // 2:r // 2 + 1]).then_inc(S["a_qf"], 1)
            act.wait_ge(S["p_v"], 1)
            a.activation(vf[:].rearrange("p (b j) d -> p b (j d)", j=2), ps[:, 0:4, 0:2 * D], ACT.Identity,
                         bias=magic_t[:], scale=rsc[:, 2:3]).then_inc(S["a_vf"], 1)
            for j in range(PAIRS):
                act.wait_ge(S["v_clip"], j + 1)
                if j >= 2:
                    act.wait_ge(S["g_at"], j - 1)
                a.activation(rnd[:, j % 2, :], pre[:, j % 2, :], ACT.Identity,
                             bias=magic_t[:]).then_inc(S["a_rnd"], 1)
            for q in range(4):
                act.wait_ge(S["p_av"], 2 * q + 2)
                a.activation(of[:, 2 * q:2 * q + 2, :].rearrange("p j d -> p (j d)"), ps[:, q, 0:2 * D],
                             ACT.Identity, bias=magic_t[:], scale=c_sc[:, 1:2]).then_inc(S["a_of"], 1)
            act.wait_ge(S["p_otr"], 1)
            a.copy(ot[:, 0, 0:T].rearrange("p (b n) -> p b n", n=NTOK),
                   ps[0:DH, 4, :].bitcast(BF16).rearrange("p (b n) -> p b n", n=64)[:, :, 0:NTOK])\
                .then_inc(S["a_ot"], 1)

            def experts(m):
                r = MOE[m]
                n, half, before = r["n"], r["hid"] // 2, r["before"]
                deviations(2 if m == 0 else 5)
                transposed(2 if m == 0 else 5)
                act.wait_ge(S["v_lg"], m + 1)
                s = slice(0, E) if m == 0 else slice(0, 1)
                a.activation(ex8[:, :, s], below[:, :, s], ACT.Exp).then_inc(S["a_ex"], 1)
                q = n // 4
                for i in range(4):
                    act.wait_ge(S["p_gt"], 8 * m + 2 * i + 1)
                    a.copy(xgt[:, 0, q * i * P:q * (i + 1) * P], ps[0:DH, 4 + 2 * (i % 2), 0:q * P])\
                        .then_inc(S["a_gt"], 1)

                def silu(j, s):
                    act.wait_ge(S["p_gu"], j * 2 + (s + 1 + 2 * before))
                    a.activation(sg[:, s, 0:half], ps[:, 2 * s, 0:half], ACT.Silu).then_inc(S["a_sg"], 1)

                def result(j, b, stored=None):
                    act.wait_ge(S["p_y"], j + (1 + before))
                    if stored is not None:
                        act.wait_ge(d_y[b], stored * 16 + 8 * before)
                    a.copy(ysb[m][:, b, :], ps[:, 4 + b, 0:D]).then_inc(S["a_y"], 1)

                silu(0, 0)
                silu(0, 1)
                for j in (1, 2):
                    silu(j, 0)
                    result(j - 1, 1 - j % 2)
                    silu(j, 1)
                with act.Fori(2, n // 2) as i:
                    for b in (1, 0):
                        j = i * 2 - b
                        silu(j, 0)
                        result(j - 1, 1 - b, i - 1)
                        silu(j, 1)
                silu(n - 1, 0)
                result(n - 2, 0, n // 2 - 1)
                silu(n - 1, 1)
                result(n - 1, 1, n // 2 - 1)

            experts(0)

            deviations(3)
            act.wait_ge(S["v_v2"], 1)
            a.activation(std[:], var2[:], ACT.Sqrt, bias=eps_t[:]).then_inc(S["a_std"], 1)
            transposed(3, padded=True, ln=ln1)
            act.wait_ge(S["g_ssm"], 1)
            for s, r in enumerate((3, 0, 1, 2)):
                act.wait_ge(S["p_in"], s + 1)
                for b in range(2):
                    a.copy(xpad[:, r, 8 * b:8 * b + 8, DC - 1:SEG],
                           ps[:, 2 * s + b, 0:HB].rearrange("p (i n) -> p i n", n=NTOK))\
                        .then_inc(S["a_cp"], 1)
            for r in range(HP):
                act.wait_ge(S["p_in"], 5 + r)
                a.activation(zs[:, r, :].rearrange("p (b n) -> p b n", b=2), two_halves(2 * r),
                             ACT.Silu).then_inc(S["a_z"], 1)
            act.wait_ge(S["v_cv"], DC)
            act.wait_ge(S["g_ssm"], 3)
            a.activation(bt[:, :, 0:NTOK], cv[0:SSN, HP], ACT.Silu).then_inc(S["a_xs"], 1)
            a.activation(ct[:, :, 0:NTOK], cv[SSN:P, HP], ACT.Silu).then_inc(S["a_xs"], 1)
            for r in range(HP):
                act.wait_ge(S["v_cv"], DC * (r + 2))
                a.activation(xst[:, r, :, 0:NTOK], cv[:, r], ACT.Silu).then_inc(S["a_xs"], 1)
            act.wait_ge(S["v_u"], 1)
            a.activation(nega[:, 0], nega[:, 2], ACT.Exp).then_inc(S["a_dt"], 1)
            act.wait_ge(S["v_u"], 2)
            a.activation(dtw[:, 2], dtw[:, 1], ACT.Exp, scale=-1.0).then_inc(S["a_dt"], 1)
            act.wait_ge(S["v_one"], 1)
            a.activation(dtw[:, 4], dtw[:, 3], ACT.Ln).then_inc(S["a_dt"], 1)
            for q in range(4):
                act.wait_ge(S["p_seg"], q + 1)
                a.activation(dec[:, 2 * q:2 * q + 2].rearrange("p j h n -> p (j h n)"),
                             ps[:, q, 0:2 * SEGW], ACT.Exp).then_inc(S["a_dec"], 1)
            act.wait_ge(S["g_ssm"], 5)
            for r in range(HP):
                act.wait_ge(S["v_yz"], r + 1)
                a.activation(ysq[:, r, 0:T], yt[:, r, 0:T], ACT.Square).then_inc(S["a_ysq"], 1)
            act.wait_ge(S["p_ssq"], 1)
            a.activation(std[:], ps[:, 6, 0:TT], ACT.Sqrt, bias=eps_t[:], scale=1.0 / DI)\
                .then_inc(S["a_std"], 1)
            deviations(4)
            transposed(4, ln=ln2)
            for r in range(HP):
                act.wait_ge(S["p_fc"], 2 * r + 2)
                a.activation(sgf[:, r, 0:T].rearrange("p (b n) -> p b n", b=2),
                             two_halves(4 * (r % 2) + 2), ACT.Silu).then_inc(S["a_fc"], 1)
            experts(1)

        @block.vector
        def _(dve):
            v = nc.vector
            chain = [0]

            def link(ins):
                chain[0] += 1
                ins.then_inc(S["v_c"], 1)
                dve.wait_ge(S["v_c"], chain[0])

            dve.wait_ge(S["d_gam"], 32)
            dve.wait_ge(S["d_wu"], 16)
            v.tensor_tensor(wug[:], wall[:, NCH:NALL, :],
                            gam[:, NCH:NALL].unsqueeze(2).broadcast_to([P, 2 * CH, D]), ALU.mult)\
                .then_inc(S["v_wug"], 1)
            dve.wait_ge(S["v_wug"], 1)
            for c in range(CH):
                dve.wait_ge(S[f"d_w{c}"], 16)
                v.tensor_tensor(weff[:, 8 * c:8 * c + 8, :], wall[:, 8 * c:8 * c + 8, :],
                                gam[:, 8 * c:8 * c + 8].unsqueeze(2).broadcast_to([P, 8, D]), ALU.mult)\
                    .then_inc(S["v_weff"], 1)
                dve.wait_ge(S["v_weff"], 3 * c + 1)
                for xh in range(2):
                    half = slice(64 * xh, 64 * xh + 64)
                    w = weff[half, 8 * c + 3 - xh:8 * c + 6 - xh:2, :]
                    v.tensor_tensor(w, w, wug[half, 2 * c:2 * c + 2, :], ALU.add).then_inc(S["v_weff"], 1)
            n_st = [0]

            def step(ins):
                n_st[0] += 1
                ins.then_inc(S["v_st"], 1)
                dve.wait_ge(S["v_st"], n_st[0])

            for c in range(CH):
                dve.wait_ge(S[f"d_x{c}"], 16)
            dve.wait_ge(S["g_const"], N_FIRST)
            step(v.tensor_tensor(xsum[:], xw[:, 0], xw[:, 1], ALU.add))
            step(v.tensor_tensor(xsum[:], xsum[:], xw[:, 2], ALU.add))
            token_sums(v, 0, xsum[:], row[:, 0], tot[:, 0], step)
            assert n_st[0] == SUMS + 2
            dve.wait_ge(S["v_weff"], 3 * CH)
            v.tensor_reduce(acc[:, 0, :], weff[:].rearrange("p c d -> p d c"), AX.X, ALU.add)\
                .then_inc(S["v_acc"], 1)
            dve.wait_ge(S["g_beta"], 1)
            v.tensor_reduce(acc[:, 1, :], wall[:].rearrange("p c d -> p d c"), AX.X, ALU.add)\
                .then_inc(S["v_acc"], 1)
            dve.wait_ge(S["v_acc"], 2)
            dve.wait_ge(S["d_att"], N_ATT)
            v.tensor_tensor(acc[0:1, 1, :], acc[0:1, 1, :], tok_b[:], ALU.add).then_inc(S["v_acc"], 1)
            dve.wait_ge(S["p_st"], 1)
            link(v.tensor_copy(mom[:].rearrange("p t s -> p (t s)"), ps[:, 4, 0:2 * TT]))
            link(v.tensor_scalar(negmu[:], mom[:, :, 0], -1.0, None, ALU.mult))
            link(v.tensor_tensor(var[:], negmu[:], negmu[:], ALU.mult))
            link(v.tensor_tensor(var[:], mom[:, :, 1], var[:], ALU.subtract))
            v.tensor_scalar(var[:], var[:], 0.0, None, ALU.max).then_inc(S["v_var"], 1)
            dve.wait_ge(S["a_std"], 1)
            link(v.reciprocal(rstd[:], std[:]))
            dve.wait_ge(S["p_tok"], 4)
            v.tensor_copy(xt[:, 1, 0:T].rearrange("p (b n) -> p b n", b=2), two_halves(2, DH))\
                .then_inc(S["v_hd"], 1)
            dve.wait_ge(S["a_s12"], 1)
            for t in range(TT):
                dve.wait_ge(S["p_ht"], t // 2 + 1)
                link(v.scalar_tensor_tensor(out=h[:, t, :], in0=s12[:, 0, :], scalar=negmu[:, t:t + 1],
                                            in1=ps[:, (6 + t // 2) % 8, (t % 2) * D:(t % 2 + 1) * D],
                                            op0=ALU.mult, op1=ALU.add))
                v.scalar_tensor_tensor(out=h[:, t, :], in0=h[:, t, :], scalar=rstd[:, t:t + 1],
                                       in1=s12[:, 1, :], op0=ALU.mult, op1=ALU.add).then_inc(S["v_h"], 1)

            def layer_norm(i, src, ready, base, stds):
                for t in range(TT):
                    dve.wait_ge(S[ready], base + t + 1)
                    v.bn_stats(st6[:, t, :], src[:, t, :]).then_inc(S["v_bn"], 1)
                for t in range(TT):
                    dve.wait_ge(S["v_bn"], TT * (i - 1) + t + 1)
                    v.bn_aggr(mv[:, t, :], st6[:, t, :]).then_inc(S["v_mv"], 1)
                dve.wait_ge(S["a_std"], stds + 1)
                dve.wait_ge(S["v_mv"], TT * i)
                link(v.reciprocal(rstd[:], std[:]))
                if i == 3:
                    link(v.tensor_tensor(var2[:], mv[:, :, 1], rstd[:], ALU.mult))
                    v.tensor_tensor(var2[:], var2[:], rstd[:], ALU.mult).then_inc(S["v_v2"], 1)
                for t in range(TT):
                    v.tensor_scalar(xn[:, t, :], src[:, t, :], mv[:, t, 0:1], rstd[:, t:t + 1],
                                    ALU.subtract, ALU.mult).then_inc(S["v_xn"], 1)

            def transposed(i, padded=False, ln=None):
                dve.wait_ge(S["p_tr"], 2 * i)
                dve.wait_ge(S["g_pad"], 2)
                src = row_of(2, 2, DH)[:, 0:T]
                dst = xt[:, 1, 0:T]
                if padded:
                    src = src.rearrange("p (b n) -> p b n", n=NTOK)
                    dst = xtp[:, 1, :, 0:NTOK]
                if ln is None:
                    v.tensor_copy(dst, src).then_inc(S["v_xt"], 1)
                else:
                    dve.wait_ge(S["d_ssm"], N_SSM)
                    v.tensor_scalar(dst, src, ln[:, 0, 1:2], ln[:, 1, 1:2], ALU.mult, ALU.add)\
                        .then_inc(S["v_xt"], 1)

            layer_norm(1, h, "v_h", 0, 1)
            transposed(1, padded=True)
            v.reciprocal(rsc[:], scales[:]).then_inc(S["v_cs"], 1)
            link(v.tensor_tensor(c_sc[:, 2:3], scales[:, 0:1], scales[:, 1:2], ALU.mult))
            v.tensor_scalar(c_sc[:, 0:1], c_sc[:, 2:3], float(HD) ** -0.5 / NTOK, None, ALU.mult)\
                .then_inc(S["v_cs"], 1)
            link(v.tensor_tensor(c_sc[:, 3:4], scales[:, 3:4], scales[:, 2:3], ALU.mult))
            dve.wait_ge(S["v_cs"], 1)
            v.tensor_tensor(c_sc[:, 1:2], c_sc[:, 3:4], rsc[:, 4:5], ALU.mult).then_inc(S["v_cs"], 1)
            dve.wait_ge(S["g_const"], N_CONST)
            for m in range(DM):
                dve.wait_ge(S["a_qf"], m + 1)
                link(v.tensor_scalar(qi[:, m, :], qf[:, m, :], MAGIC, QLO, ALU.subtract, ALU.max))
                for hh in range(HH):
                    v.tensor_scalar(qe[:, m, :, hh, :], qi[:, m, :].rearrange("p (b n) -> p b n", n=NTOK),
                                    QHI, head_mask[:, hh:hh + 1], ALU.min, ALU.mult).then_inc(S["v_qe"], 1)
            dve.wait_ge(S["g_pad"], 6)
            for m in range(DM):
                dve.wait_ge(S["a_qf"], m + 3)
                link(v.tensor_scalar(kc[:, m, :], qf[:, 2 + m, :], MAGIC, QLO, ALU.subtract, ALU.max))
                v.tensor_scalar(ki[:, m, :, 0:NTOK], kc[:, m, :].rearrange("p (b n) -> p b n", n=NTOK),
                                QHI, None, ALU.min).then_inc(S["v_ki"], 1)

            def values():
                dve.wait_ge(S["a_vf"], 1)
                link(v.tensor_scalar(vc[:], vf[:], MAGIC, QLO, ALU.subtract, ALU.max))
                for i in range(2):
                    r = slice(64 * i, 64 * i + 64)
                    v.tensor_scalar(vi[r, i], vc[r], QHI, None, ALU.min).then_inc(S["v_vi"], 1)

            dve.wait_ge(S["v_cs"], 3)
            for j in range(PAIRS):
                dve.wait_ge(S["p_sc"], j + 1)
                if j >= 2:
                    dve.wait_ge(S["a_rnd"], j - 1)
                v.tensor_scalar(pre[:, j % 2, :], ps[:, 4 + j % 4, 0:W2], c_sc[:, 0:1], rsc[:, 3:4],
                                ALU.mult, ALU.mult).then_inc(S["v_pre"], 1)
                dve.wait_ge(S["v_pre"], j + 1)
                v.tensor_scalar(pre[:, j % 2, :], pre[:, j % 2, :], 0.0, AHI, ALU.max, ALU.min)\
                    .then_inc(S["v_clip"], 1)
                if j == 0:
                    values()
            for q in range(4):
                dve.wait_ge(S["a_of"], q + 1)
                j2 = slice(2 * q, 2 * q + 2)
                link(v.tensor_scalar(oc[:, j2], of[:, j2], MAGIC, QLO, ALU.subtract, ALU.max))
                v.tensor_scalar(oi[:, j2], oc[:, j2], QHI, None, ALU.min).then_inc(S["v_oi"], 1)
            dve.wait_ge(S["p_otr"], 2)
            v.tensor_copy(ot[:, 1, 0:T].rearrange("p (b n) -> p b n", n=NTOK),
                          ps[0:DH, 5, :].bitcast(BF16).rearrange("p (b n) -> p b n", n=64)[:, :, 0:NTOK])\
                .then_inc(S["v_ot"], 1)
            dve.wait_ge(S["g_hb"], 1)
            for t in range(TT):
                dve.wait_ge(S["p_proj"], min(t | 1, TT - 1) + 1)
                v.scalar_tensor_tensor(out=h[:, t, :], in0=ps[:, t // 2, (t % 2) * D:(t % 2 + 1) * D],
                                       scalar=scales[:, 4:5], in1=hb[:, t, :], op0=ALU.mult, op1=ALU.add)\
                    .then_inc(S["v_h"], 1)

            def experts(m):
                r = MOE[m]
                n, half, before, K = r["n"], r["hid"] // 2, r["before"], r["k"]
                i_ln = 2 if m == 0 else 5
                layer_norm(i_ln, h, "v_h", TT * (1 if m == 0 else 3), 2 if m == 0 else 7)
                transposed(i_ln)
                dve.wait_ge(S["p_lg"], m + 1)
                lg = ps[:, 6, 0:TT * E].rearrange("p (t e) -> p t e", e=E)
                if m == 0:
                    link(v.tensor_tensor(logit[:], lg, rb1[:].unsqueeze(1).broadcast_to([P, TT, E]), ALU.add))
                else:
                    link(v.tensor_copy(logit[:], lg))
                for t in range(TT):
                    link(v.max(top8[:, t, :], logit[:, t, :]))
                for t in range(TT):
                    link(v.max_index(idx8[:, t, :], top8[:, t, :], logit[:, t, :]))
                link(v.tensor_copy(idxf[:], idx8[:, :, 0:2]))
                for k in range(K):
                    link(v.tensor_tensor(oh[:, k], idxf[:, :, k:k + 1].broadcast_to([P, TT, E]),
                                         iota_e[:].unsqueeze(1).broadcast_to([P, TT, E]), ALU.is_equal))
                if K == 1:
                    v.tensor_copy(ohb[:], oh[:, 0]).then_inc(S["v_oh"], 1)
                    v.tensor_tensor(below[:], logit[:], top8[:, :, 0:1].broadcast_to([P, TT, E]),
                                    ALU.subtract).then_inc(S["v_lg"], 1)
                else:
                    v.tensor_tensor(ohb[:], oh[:, 0], oh[:, 1], ALU.add).then_inc(S["v_oh"], 1)
                    v.tensor_tensor(below[:, :, 0:1], top8[:, :, 1:2], top8[:, :, 0:1],
                                    ALU.subtract).then_inc(S["v_lg"], 1)
                dve.wait_ge(S["p_rk"], m + 1)
                link(v.tensor_scalar(tiles_e[:], ps[:, 7, TT * E:TT * E + E], (P - 1) / 2, 1.0 / P,
                                     ALU.add, ALU.mult))
                link(v.tensor_scalar(tiles_e[:], tiles_e[:], MAGIC, MAGIC, ALU.add, ALU.subtract))
                link(v.tensor_tensor_scan(cum_e[:], ones8[:], tiles_e[:], 0.0, ALU.mult, ALU.add))
                link(v.tensor_tensor(teb[:, 0:n, :], cum_e[0:1, :].unsqueeze(1).broadcast_to([1, n, E]),
                                     iota_t[:, 0:n, :], ALU.is_le))
                link(v.tensor_reduce(tef[:, 0:n], teb[:, 0:n, :], AX.X, ALU.add))
                v.tensor_scalar(te[:, 0:n], tef[:, 0:n], float(E - 1), None, ALU.min).then_inc(S["v_te"], 1)
                link(v.tensor_tensor(base_e[:], cum_e[:], tiles_e[:], ALU.subtract))
                link(v.tensor_scalar(base_e[:], base_e[:], float(P), None, ALU.mult))
                link(v.tensor_tensor(rank_b[:], ps[:, 7, 0:TT * E].rearrange("p (t e) -> p t e", e=E),
                                     base_e[:].unsqueeze(1).broadcast_to([P, TT, E]), ALU.add))
                for k in range(K):
                    link(v.tensor_tensor(pick[:, k], rank_b[:], oh[:, k], ALU.mult))
                    link(v.tensor_reduce(slotf[:, k], pick[:, k], AX.X, ALU.add))
                v.tensor_copy(slot[:, 0:K], slotf[:, 0:K]).then_inc(S["v_slot"], 1)
                dve.wait_ge(S["a_ex"], m + 1)
                if K == 1:
                    link(v.tensor_reduce(gsum[:], ex8[:], AX.X, ALU.add))
                    link(v.reciprocal(gate[:, 0], gsum[:]))
                else:
                    link(v.tensor_scalar(gsum[:], ex8[:, :, 0], 1.0, None, ALU.add))
                    link(v.reciprocal(gate[:, 0], gsum[:]))
                    link(v.tensor_tensor(gate[:, 1], gate[:, 0], ex8[:, :, 0], ALU.mult))
                q = n // 4
                for i in range(4):
                    dve.wait_ge(S["p_gt"], 8 * m + 2 * i + 2)
                    v.tensor_copy(xgt[:, 1, q * i * P:q * (i + 1) * P], ps[0:DH, 5 + 2 * (i % 2), 0:q * P])\
                        .then_inc(S["v_gt"], 1)

                def product(j, s):
                    dve.wait_ge(S["a_sg"], j * 2 + (s + 1 + 2 * before))
                    v.tensor_tensor(ht[:, s, 0:half], sg[:, s, 0:half], ps[:, 2 * s + 1, 0:half], ALU.mult)\
                        .then_inc(S["v_ht"], 1)

                with dve.Fori(0, n // 2) as i:
                    for b in range(2):
                        for s in range(2):
                            product(i * 2 + b, s)
                for t in range(TT):
                    rows = P if t < TT - 1 else LAST
                    dve.wait_ge(S["d_yg"], 16 * (TT * (1 if m else 0) + TT * K))
                    for k in range(K):
                        v.scalar_tensor_tensor(out=h[0:rows, t, :], in0=yg[m][0:rows, k, t, :],
                                               scalar=gate[0:rows, k, t:t + 1], in1=h[0:rows, t, :],
                                               op0=ALU.mult, op1=ALU.add).then_inc(S["v_h"], 1)
                        if K == 2 and k == 0:
                            dve.wait_ge(S["v_h"], 4 * TT + 2 * t + 1)

            experts(0)

            layer_norm(3, h, "v_h", 2 * TT, 3)
            dve.wait_ge(S["a_std"], 5)
            link(v.reciprocal(rstd2[:], std[:]))
            for t in range(TT):
                dve.wait_ge(S["v_xn"], 2 * TT + t + 1)
                v.tensor_scalar(xn2[:, t, :], xn[:, t, :], rstd2[:, t:t + 1], None, ALU.mult)\
                    .then_inc(S["v_xn"], 1)
            transposed(3, padded=True, ln=ln1)
            n_cv = 0
            for s, r in enumerate((3, 0, 1, 2)):
                dve.wait_ge(S["a_cp"], 2 * s + 2)
                for k in range(DC):
                    x = xpad[:, r, :, k:k + NTOK]
                    if k == 0:
                        ins = v.tensor_scalar(cv[:, r], x, convw[:, r, 0:1], convb[:, r:r + 1], ALU.mult, ALU.add)
                    else:
                        ins = v.scalar_tensor_tensor(out=cv[:, r], in0=x, scalar=convw[:, r, k:k + 1],
                                                     in1=cv[:, r], op0=ALU.mult, op1=ALU.add)
                    n_cv += 1
                    ins.then_inc(S["v_cv"], 1)
                    dve.wait_ge(S["v_cv"], n_cv)
            v.tensor_scalar(nega[:, 2], alog[:], 88.7, None, ALU.min).then_inc(S["v_u"], 1)
            dve.wait_ge(S["p_dt"], 1)
            link(v.tensor_tensor(dtw[:, 0], ps[:, 6, 0:PAIRS * SSH].rearrange("p (j h) -> p j h", h=SSH),
                                 dtb[:].unsqueeze(1).broadcast_to([P, PAIRS, SSH]), ALU.add))
            v.scalar_tensor_tensor(out=dtw[:, 1].rearrange("p j h -> p (j h)"),
                                   in0=dtw[:, 0].rearrange("p j h -> p (j h)"), scalar=-1.0,
                                   in1=dtw[:, 0].rearrange("p j h -> p (j h)"), op0=ALU.mult, op1=ALU.max)\
                .then_inc(S["v_u"], 1)
            dve.wait_ge(S["a_dt"], 2)
            v.tensor_scalar(dtw[:, 3], dtw[:, 2], 1.0, None, ALU.add).then_inc(S["v_one"], 1)
            dve.wait_ge(S["v_one"], 1)
            link(v.reciprocal(dtw[:, 5], dtw[:, 3]))
            link(v.tensor_scalar(dtw[:, 6], dtw[:, 3], -1.0, None, ALU.add))
            link(v.tensor_tensor(dtw[:, 6], dtw[:, 2], dtw[:, 6], ALU.subtract))
            link(v.tensor_tensor(dtw[:, 6], dtw[:, 6], dtw[:, 5], ALU.mult))
            dve.wait_ge(S["a_dt"], 3)
            link(v.tensor_tensor(dtw[:, 6], dtw[:, 6], dtw[:, 4], ALU.add))
            link(v.scalar_tensor_tensor(out=dtw[:, 7].rearrange("p j h -> p (j h)"),
                                        in0=dtw[:, 0].rearrange("p j h -> p (j h)"), scalar=0.0,
                                        in1=dtw[:, 6].rearrange("p j h -> p (j h)"), op0=ALU.max, op1=ALU.add))
            link(v.tensor_scalar(nega[:, 1], nega[:, 0], 1e30, None, ALU.min))
            link(v.tensor_tensor(dtw[:, 1], dtw[:, 7], nega[:, 1].unsqueeze(1).broadcast_to([P, PAIRS, SSH]),
                                 ALU.mult))
            link(v.tensor_scalar(dtw[:, 3], dtw[:, 7], 1.0, None, ALU.min))
            link(v.tensor_tensor(dtw[:, 3], dtw[:, 3], nega[:, 0].unsqueeze(1).broadcast_to([P, PAIRS, SSH]),
                                 ALU.mult))
            link(v.tensor_tensor(dtw[:, 1], dtw[:, 1], dtw[:, 3], ALU.max))
            link(v.tensor_scalar(dtw[:, 1], dtw[:, 1], 200.0, -1.0, ALU.min, ALU.mult))
            v.tensor_tensor(av[:].rearrange("p j h n -> p (j h) n"),
                            dtw[:, 1].rearrange("p j h -> p (j h)").unsqueeze(2)
                            .broadcast_to([P, PAIRS * SSH, NTOK]),
                            upto[:].unsqueeze(1).broadcast_to([P, PAIRS * SSH, NTOK]), ALU.mult)\
                .then_inc(S["v_av"], 1)
            dve.wait_ge(S["p_g"], 1)
            v.tensor_tensor(gm[:], ps[:, 7, 0:PAIRS * NTOK].rearrange("p (j n) -> p j n", n=NTOK)
                            .unsqueeze(2).broadcast_to([P, PAIRS, 2, NTOK]),
                            causal[:].unsqueeze(1).broadcast_to([P, PAIRS, 2, NTOK]), ALU.mult)\
                .then_inc(S["v_gm"], 1)
            for j in range(PAIRS):
                dve.wait_ge(S["p_xs"], j + 1)
                v.tensor_tensor(dtx[:, j, :].rearrange("p (h d) -> p h d", d=SSD),
                                ps[:, 4 + j % 2, 0:DI].rearrange("p (h d) -> p h d", d=SSD),
                                dtw[:, 7, j, :].unsqueeze(2).broadcast_to([P, SSH, SSD]), ALU.mult)\
                    .then_inc(S["v_dtx"], 1)
            dve.wait_ge(S["v_gm"], 1)
            for j in range(PAIRS):
                dve.wait_ge(S["a_dec"], j // 2 + 1)
                v.tensor_tensor(mix[:, j], dec[:, j].unsqueeze(2).broadcast_to([P, SSH, 2, NTOK]),
                                gm[:, j].unsqueeze(1).broadcast_to([P, SSH, 2, NTOK]), ALU.mult)\
                    .then_inc(S["v_mix"], 1)
            dve.wait_ge(S["p_ys"], 1)
            dve.wait_ge(S["g_ssm"], 4)
            dve.wait_ge(S["a_xs"], 5)
            for r in range(HP):
                for b in range(2):
                    v.scalar_tensor_tensor(
                        out=yt[:, r, HB * b:HB * b + HB].rearrange("p (i n) -> p i n", n=NTOK),
                        in0=xst[:, r, 8 * b:8 * b + 8, 0:NTOK], scalar=dskip[:, r:r + 1],
                        in1=ps[:, 2 * r + b, 0:HB].rearrange("p (i n) -> p i n", n=NTOK),
                        op0=ALU.mult, op1=ALU.add).then_inc(S["v_ys"], 1)
                dve.wait_ge(S["v_ys"], 2 * r + 2)
                dve.wait_ge(S["a_z"], r + 1)
                v.tensor_tensor(yt[:, r, 0:T], yt[:, r, 0:T], zs[:, r, :], ALU.mult).then_inc(S["v_yz"], 1)
            dve.wait_ge(S["a_std"], 6)
            link(v.reciprocal(rstd[:], std[:]))
            for t in range(TT):
                dve.wait_ge(S["p_out"], min(t | 1, TT - 1) + 1)
                v.scalar_tensor_tensor(out=x2[:, t, :], in0=ps[:, t // 2, (t % 2) * D:(t % 2 + 1) * D],
                                       scalar=rstd[:, t:t + 1], in1=xn[:, t, :], op0=ALU.mult, op1=ALU.add)\
                    .then_inc(S["v_x2"], 1)
            layer_norm(4, x2, "v_x2", 0, 6)
            transposed(4, ln=ln2)
            for r in range(HP):
                dve.wait_ge(S["a_fc"], r + 1)
                v.tensor_tensor(ft[:, r, 0:T].rearrange("p (b n) -> p b n", b=2), two_halves(4 * (r % 2)),
                                sgf[:, r, 0:T].rearrange("p (b n) -> p b n", b=2), ALU.mult)\
                    .then_inc(S["v_fc"], 1)
            dve.wait_ge(S["g_hb"], 2)
            for t in range(TT):
                dve.wait_ge(S["p_f2"], min(t | 1, TT - 1) + 1)
                v.tensor_tensor(h[:, t, :], ps[:, 4 + t // 2, (t % 2) * D:(t % 2 + 1) * D], hb[:, t, :],
                                ALU.add).then_inc(S["v_h"], 1)
            experts(1)

        @block.tensor
        def _(pe):
            mm = nc.tensor.matmul

            for c in range(CH):
                pe.wait_ge(S[f"d_x{c}"], 16)
                pe.wait_ge(S["v_weff"], 3 * c + 3)
                for yh in range(2):
                    for win in range(4):
                        wy, wx = win // 2, win % 2
                        first, last = (c, yh, win) == (0, 0, 0), (c, yh, win) == (CH - 1, 1, 3)
                        img = xw[:, c, yh].rearrange("p (b r x) -> p b r x", r=WIN, x=WIN)
                        for m in range(DM):
                            for b in range(2):
                                ins = mm(ps[0:DH, 2 * m + b, 0:HB],
                                         weff[:, 8 * c + 4 * yh + win, DH * m:DH * m + DH],
                                         img[:, 8 * b:8 * b + 8, wy:wy + GRID, wx:wx + GRID],
                                         start=first, stop=last)
                                if last:
                                    ins.then_inc(S["p_tok"], 1)
            pe.wait_ge(S["v_st"], SUMS + 2)
            pe.wait_ge(S["g_sq"], SUMS + 2)
            pe.wait_ge(S["g_const"], N_FIRST)
            for t in range(TT):
                for s in range(2):
                    ins = mm(ps[:, 4, 2 * t + s:2 * t + s + 1], tot[:, s, t * P:t * P + P], inv_k[:],
                             start=True, stop=True)
            ins.then_inc(S["p_st"], 1)
            for s in range(2):
                pe.wait_ge(S["v_acc"], 1 if s == 0 else 3)
                mm(ps[:, 5, s * D:s * D + D], ones[:], acc[:, s, :], start=True, stop=True)\
                    .then_inc(S["p_st"], 1)
            pe.wait_ge(S["a_hd"], 1)
            pe.wait_ge(S["v_hd"], 1)
            pe.wait_ge(S["g_pad"], 1)
            for t in range(TT):
                for m in range(DM):
                    ins = nc.tensor.transpose(
                        ps[:, (6 + t // 2) % 8, (t % 2) * D + m * DH:(t % 2) * D + (m + 1) * DH],
                        xt[:, m, t * P:t * P + P], ident[0:DH, 0:DH])
                if t % 2 == 1 or t == TT - 1:
                    ins.then_inc(S["p_ht"], 1)

            def transposes(i, src, count):
                for t in range(TT):
                    pe.wait_ge(S["v_xn"], count + t + 1)
                    for m in range(DM):
                        ins = nc.tensor.transpose(row_of(2 * m, 2, DH)[:, t * P:t * P + P],
                                                  src[:, t, m * DH:m * DH + DH], ident[:])
                        if t == TT - 1:
                            ins.then_inc(S["p_tr"], 1)
                pe.wait_ge(S["a_xt"], i)
                pe.wait_ge(S["v_xt"], i)

            def windows(m, b):
                return xtp[:, m, 8 * b:8 * b + 8, 0:NTOK]

            transposes(1, xn, 0)
            pe.wait_ge(S["d_att"], N_ATT)
            for r in range(4):
                for m in range(DM):
                    for b in range(2):
                        ins = mm(ps[0:DH, 2 * r + b, 0:HB], wqkv[:, m, DH * r:DH * r + DH], windows(m, b),
                                 start=(m == 0), stop=(m == 1))
                ins.then_inc(S["p_qk"], 1)
            pe.wait_ge(S["a_qf"], 2)
            for j in range(PAIRS):
                for m in range(DM):
                    ins = mm(ps[:, j // 2, (j % 2) * D:(j % 2 + 1) * D],
                             xtp[:, m, 2 * j:2 * j + 2, :].rearrange("p i n -> p (i n)"),
                             wqkv[:, m, 2 * D:3 * D], start=(m == 0), stop=(m == 1))
            ins.then_inc(S["p_v"], 1)

            def scores(j):
                if j == 0:
                    pe.wait_ge(S["v_qe"], 2 * HH)
                    pe.wait_ge(S["v_ki"], 2)
                    pe.wait_ge(S["a_qf"], 4)
                if j >= 4:
                    pe.wait_ge(S["v_pre"], j - 3)
                for i in range(2):
                    for m in range(DM):
                        ins = mm(ps[64 * i:64 * i + 64, 4 + j % 4, m * HH * NTOK:(m + 1) * HH * NTOK],
                                 ki[:, m, 2 * j + i, :],
                                 qe[:, m, 2 * j + i].rearrange("p h n -> p (h n)"), start=True, stop=True)
                ins.then_inc(S["p_sc"], 1)

            def attend(j):
                if j == 0:
                    pe.wait_ge(S["v_vi"], 2)
                    pe.wait_ge(S["a_vf"], 1)
                pe.wait_ge(S["g_at"], j + 1)
                for i in range(2):
                    for hh in range(HEADS):
                        ins = mm(ps[64 * i:64 * i + 64, j // 2, (j % 2) * D + hh * HD:(j % 2) * D + (hh + 1) * HD],
                                 at[:, j % 2, hh * NTOK:hh * NTOK + 64], vi[:, i, j, hh * HD:(hh + 1) * HD],
                                 start=True, stop=True)
                ins.then_inc(S["p_av"], 1)

            for j in range(PAIRS + 2):
                if j < PAIRS:
                    scores(j)
                if j >= 2:
                    attend(j - 2)
            for m in range(DM):
                for j in range(PAIRS):
                    pe.wait_ge(S["v_oi"], j // 2 + 1)
                    ins = nc.tensor.transpose(ps[0:DH, 4 + m, :].bitcast(BF16)[:, j * P:j * P + P],
                                              oi[:, j, m * DH:m * DH + DH], identb[:])
                ins.then_inc(S["p_otr"], 1)
            pe.wait_ge(S["a_ot"], 1)
            pe.wait_ge(S["v_ot"], 1)
            for t in range(TT):
                for m in range(DM):
                    ins = mm(ps[:, t // 2, (t % 2) * D:(t % 2 + 1) * D], ot[:, m, t * P:t * P + P],
                             wproj[:, m, :], start=(m == 0), stop=(m == 1))
                ins.then_inc(S["p_proj"], 1)

            def experts(m_):
                r = MOE[m_]
                n, hid, before = r["n"], r["hid"], r["before"]
                tiles = hid // P // 2
                transposes(2 if m_ == 0 else 5, xn, TT if m_ == 0 else 5 * TT)
                for t in range(TT):
                    for m in range(DM):
                        ins = mm(ps[:, 6, t * E:t * E + E], xt[:, m, t * P:t * P + P], rw[m_][:, m, :],
                                 start=(m == 0), stop=(m == 1))
                ins.then_inc(S["p_lg"], 1)
                pe.wait_ge(S["v_oh"], m_ + 1)
                for t in range(TT):
                    for u in range(t):
                        mm(ps[:, 7, t * E:t * E + E], onesb[:], ohb[:, u, :], start=(u == 0), stop=False)
                    mm(ps[:, 7, t * E:t * E + E], earlier[:], ohb[:, t, :], start=(t == 0), stop=True)
                for t in range(TT):
                    k = P if t < TT - 1 else LAST
                    ins = mm(ps[:, 7, TT * E:TT * E + E], onesb[0:k, :], ohb[0:k, t, :], start=(t == 0),
                             stop=(t == TT - 1))
                ins.then_inc(S["p_rk"], 1)
                q = n // 4
                for i in range(4):
                    pe.wait_ge(S[f"d_xg{i}"], 16 * (m_ + 1))
                    if i >= 2:
                        pe.wait_ge(S["a_gt"], 4 * m_ + i - 1)
                        pe.wait_ge(S["v_gt"], 4 * m_ + i - 1)
                    for m in range(DM):
                        for c in range(q):
                            ins = nc.tensor.transpose(ps[0:DH, 4 + 2 * (i % 2) + m, c * P:c * P + P],
                                                      xg[:, q * i + c, m * DH:m * DH + DH], ident[:])
                        ins.then_inc(S["p_gt"], 1)
                pe.wait_ge(S["a_gt"], 4 * m_ + 4)
                pe.wait_ge(S["v_gt"], 4 * m_ + 4)

                def up(j, b, s, wait=True):
                    if s == 0:
                        pe.wait_ge(d_w12[b], (j + (2 - b)) * 8 + 8 * before)
                    if wait:
                        pe.wait_ge(S["v_ht"], j * 2 + (s - 1 + 2 * before))
                    for g in range(2):
                        for c in range(tiles):
                            col = g * hid + (s * tiles + c) * P
                            for m in range(DM):
                                ins = mm(ps[:, 2 * s + g, c * P:c * P + P], w12[b][:, m, col:col + P],
                                         xgt[:, m, bass.ds(j * P, P)], start=(m == 0), stop=(m == 1))
                    ins.then_inc(S["p_gu"], 1)

                def down(j, b, s, wait=True):
                    pe.wait_ge(S["v_ht"], j * 2 + (s + 1 + 2 * before))
                    if s == 0:
                        pe.wait_ge(d_w3[b], (j + (2 - b)) * 8 + 8 * before)
                    if s == 0 and wait:
                        pe.wait_ge(S["a_y"], j + (before - 1))
                    for c in range(tiles):
                        ins = mm(ps[:, 4 + b, 0:D], ht[:, s, c * P:c * P + P], w3[b][:, s * tiles + c, :],
                                 start=(s == 0 and c == 0), stop=(s == 1 and c == tiles - 1))
                    if s == 1:
                        ins.then_inc(S["p_y"], 1)

                up(0, 0, 0, wait=False)
                up(0, 0, 1, wait=False)
                down(0, 0, 0, wait=False)
                for j in (1, 2):
                    up(j, j % 2, 0)
                    down(j - 1, 1 - j % 2, 1)
                    up(j, j % 2, 1)
                    down(j, j % 2, 0, wait=(j == 2))
                with pe.Fori(2, n // 2) as i:
                    for b in (1, 0):
                        j = i * 2 - b
                        up(j, b, 0)
                        down(j - 1, 1 - b, 1)
                        up(j, b, 1)
                        down(j, b, 0)
                up(n - 1, 1, 0)
                down(n - 2, 0, 1)
                up(n - 1, 1, 1)
                down(n - 1, 1, 0)
                down(n - 1, 1, 1)

            experts(0)

            transposes(3, xn2, 3 * TT)
            cols = (2 * DI, DI, DI + P, DI + 2 * P, 0, P, 2 * P)
            for s, c0 in enumerate(cols):
                if s >= 4:
                    pe.wait_ge(S["a_cp"], 2 * (s - 3))
                for m in range(DM):
                    for b in range(2):
                        ins = mm(ps[:, 2 * (s % 4) + b, 0:HB], inproj[:, m, c0:c0 + P], windows(m, b),
                                 start=(m == 0), stop=(m == 1))
                ins.then_inc(S["p_in"], 1)
            pe.wait_ge(S["a_cp"], 8)
            for j in range(PAIRS):
                for m in range(DM):
                    ins = mm(ps[:, 6, j * SSH:j * SSH + SSH],
                             xtp[:, m, 2 * j:2 * j + 2, :].rearrange("p i n -> p (i n)"),
                             inproj[:, m, 2 * DI + 2 * SSN:], start=(m == 0), stop=(m == 1))
            ins.then_inc(S["p_dt"], 1)
            pe.wait_ge(S["a_xs"], 2)
            for b in range(IMGS):
                i = b % 2
                ins = mm(ps[64 * i:64 * i + 64, 7, (b // 2) * NTOK:(b // 2 + 1) * NTOK], bt[:, b, :],
                         ct[:, b, 0:NTOK], start=True, stop=True)
            ins.then_inc(S["p_g"], 1)
            pe.wait_ge(S["a_xs"], 5)
            pe.wait_ge(S["a_z"], 3)
            for j in range(PAIRS):
                if j >= 2:
                    pe.wait_ge(S["v_dtx"], j - 1)
                for r in range(HP):
                    ins = nc.tensor.transpose(ps[:, 4 + j % 2, r * P:r * P + P],
                                              xst[:, r, 2 * j:2 * j + 2, :].rearrange("p i n -> p (i n)"),
                                              ident[:])
                ins.then_inc(S["p_xs"], 1)
                if j == 1:
                    pe.wait_ge(S["v_av"], 1)
                    for jj in range(PAIRS):
                        ins = mm(ps[:, jj // 2, (jj % 2) * SEGW:(jj % 2 + 1) * SEGW], later_blk[:],
                                 av[:, jj].rearrange("p h n -> p (h n)"), start=True, stop=True)
                        if jj % 2 == 1:
                            ins.then_inc(S["p_seg"], 1)
            pe.wait_ge(S["a_dec"], 4)
            pe.wait_ge(S["v_dtx"], PAIRS)
            for j in range(PAIRS):
                pe.wait_ge(S["v_mix"], j + 1)
                for hh in range(SSH):
                    o = 64 * (hh % 2)
                    ins = mm(ps[o:o + 64, 2 * (hh // 2) + j // 4, (j % 4) * 2 * NTOK:(j % 4 + 1) * 2 * NTOK],
                             dtx[:, j, hh * SSD:(hh + 1) * SSD], mix[:, j, hh].rearrange("p i n -> p (i n)"),
                             start=True, stop=True)
            ins.then_inc(S["p_ys"], 1)
            pe.wait_ge(S["g_ssm"], 5)
            pe.wait_ge(S["a_ysq"], HP)
            for t in range(TT):
                for r in range(HP):
                    ins = mm(ps[:, 6, t:t + 1], ysq[:, r, t * P:t * P + P], ones[:, 0:1], start=(r == 0),
                             stop=(r == HP - 1))
            ins.then_inc(S["p_ssq"], 1)
            pe.wait_ge(S["v_ys"], 2 * HP)
            pe.wait_ge(S["g_wout"], 1)
            for t in range(TT):
                for r in range(HP):
                    ins = mm(ps[:, t // 2, (t % 2) * D:(t % 2 + 1) * D], yt[:, r, t * P:t * P + P],
                             outproj[:, r, :], start=(r == 0), stop=(r == HP - 1))
                ins.then_inc(S["p_out"], 1)
            transposes(4, xn, 4 * TT)
            for r in range(HP):
                if r == 2:
                    pe.wait_ge(S["v_fc"], 1)
                for g in range(2):
                    for m in range(DM):
                        for b in range(2):
                            ins = mm(ps[:, 4 * (r % 2) + 2 * g + b, 0:HB],
                                     fc1[:, m, g * DI + r * P:g * DI + r * P + P],
                                     xt[:, m, HB * b:HB * b + HB], start=(m == 0), stop=(m == 1))
                    ins.then_inc(S["p_fc"], 1)
            pe.wait_ge(S["v_fc"], HP)
            for t in range(TT):
                for r in range(HP):
                    ins = mm(ps[:, 4 + t // 2, (t % 2) * D:(t % 2 + 1) * D], ft[:, r, t * P:t * P + P],
                             fc2[:, r, :], start=(r == 0), stop=(r == HP - 1))
                ins.then_inc(S["p_f2"], 1)
            experts(1)


def _halves(w):
    return w.reshape(DM, DH, -1).transpose(1, 0, 2)


def _chunks(w):
    return w.reshape(-1, P, w.shape[-1]).transpose(1, 0, 2)


def _patch_rows(w):
    n = w.shape[0]
    w = w.reshape(n, 2, 8, 2, 8, 5, CH)
    sh = np.stack([w[..., s, :] for s in (1, 3, 4, 2)])
    sh = sh.transpose(4, 3, 5, 6, 2, 0, 1)
    sh = sh.reshape(P, NCH, n)
    un = w[..., 0, :]
    un = un[:, ::-1, :, ::-1]
    un = un.transpose(3, 2, 4, 5, 1, 0).reshape(P, CH * 2, n)
    return sh, un


def _rows(w):
    return np.broadcast_to(w.reshape(1, -1), (P, w.size))


def kernel(**inputs):
    import concourse.bacc as bacc
    from concourse.bass_utils import run_bass_kernel_spmd

    x = {k: np.asarray(v) for k, v in inputs.items()}
    a = {}
    img = np.pad(x["x"], ((0, 0), (0, 0), (8, 8), (8, 8))).reshape(IMGS, CH, WIN, 2, 8, WIN, 2, 8)
    a["xw"] = img.transpose(6, 4, 7, 1, 3, 0, 2, 5).reshape(P, CH, 2, NWIN)
    a["w_sh"], a["w_un"] = _patch_rows(x["L0_tok_W"])
    for name, src in (("gam", "L0_tok_ln_gamma"), ("bet", "L0_tok_ln_beta")):
        sh, un = _patch_rows(x[src].reshape(1, -1))
        a[name] = np.concatenate([sh, un], axis=1)[:, :, 0]
    a["tok_b"] = x["L0_tok_b"].reshape(1, D)
    a["wqkv"] = _halves(x["L0_attn_Wqkv"].T)
    a["wproj"] = _halves(x["L0_attn_Wproj"].T)
    a["bproj"] = _rows(x["L0_attn_bproj"])
    a["scales"] = _rows(np.stack([x["L0_attn_s_" + s].reshape(()) for s in ("q", "k", "v", "attn", "after")]))
    a["rw1"] = _halves(x["L0_ffn_router_w"])
    a["rb1"] = _rows(x["L0_ffn_router_b"])
    a["rw2"] = _halves(x["L1_ffn_router_w"].T)
    a["m1_w12"] = np.concatenate([x["L0_ffn_w1"], x["L0_ffn_w2"]], axis=2)\
        .reshape(E, DM, DH, 2 * M1_H).transpose(0, 2, 1, 3)
    a["m1_w3"] = x["L0_ffn_w3"].reshape(E, M1_H // P, P, D).transpose(0, 2, 1, 3)
    a["m2_w12"] = np.concatenate([x["L1_ffn_Wg"], x["L1_ffn_Wu"]], axis=1).transpose(0, 2, 1)\
        .reshape(E, DM, DH, 2 * M2_H).transpose(0, 2, 1, 3)
    a["m2_w3"] = x["L1_ffn_Wd"].transpose(0, 2, 1).reshape(E, M2_H // P, P, D).transpose(0, 2, 1, 3)
    L = "L1_attn_"
    a["inproj"] = _halves(x[L + "in_proj_w"].T)
    a["convw"] = _chunks(x[L + "conv_w"])
    a["convb"] = x[L + "conv_b"].reshape(HP + 1, P).T
    a["dskip"] = np.repeat(x[L + "D_skip"], SSD).reshape(HP, P).T
    a["dtb"] = _rows(x[L + "dt_bias"])
    a["alog"] = _rows(x[L + "A_log"])
    a["normw"] = x[L + "ssm_norm_w"].reshape(HP, P).T
    a["outproj"] = _chunks(x[L + "out_proj_w"].T)
    a["fc1"] = _halves(x[L + "fc1_w"].T)
    a["fc2"] = _chunks(x[L + "fc2_w"].T)
    for i in (1, 2):
        a[f"ln{i}"] = np.stack([x[L + f"ln{i}_w"].reshape(DM, DH).T, x[L + f"ln{i}_b"].reshape(DM, DH).T], axis=1)

    nc = bacc.Bacc("TRN2", target_bir_lowering=False, num_devices=1)
    arrays, aps = {}, {}
    for name, arr in a.items():
        arrays["in_" + name] = np.ascontiguousarray(arr)
        aps[name] = nc.dram_tensor("in_" + name, arr.shape, mybir.dt.from_np(arr.dtype),
                                   kind="ExternalInput").ap()
    out = nc.dram_tensor("out_h", (T, D), F32, kind="ExternalOutput").ap()
    build(nc, aps, out)
    r = run_bass_kernel_spmd(nc, [arrays], core_ids=[0])
    return r.results[0]["out_h"].reshape(IMGS, NTOK, D)
```

```python
from contextlib import ExitStack

import numpy as np
import concourse.bass as bass
from concourse import mybir

ALU = mybir.AluOpType
ACT = mybir.ActivationFunctionType
F32 = mybir.dt.float32
BF16 = mybir.dt.bfloat16
I32 = mybir.dt.int32
U32 = mybir.dt.uint32
AX = mybir.AxisListType

P = 128
IMGS, CH, SIDE, PATCH = 16, 3, 96, 16
GRID = SIDE // PATCH
NTOK = GRID * GRID
T = IMGS * NTOK
TT = (T + P - 1) // P
TPAD = TT * P
LAST = T - (TT - 1) * P
D, DH, DM = 192, 96, 2
HB = IMGS // 2 * NTOK
WIN = GRID + 1
NWIN = IMGS * WIN * WIN
NCH = CH * 2 * 4
NALL = NCH + CH * 2
RING = 12
KTOK = PATCH * PATCH * CH * 5
PAIRS = IMGS // 2
HEADS, HD = 12, 16
HH = HEADS // 2
QLO, QHI, AHI = -4.0, 3.0, 7.0
MAGIC = 12582912.0
EPS = 1e-5
E = 8
SSH, SSD, SSN = 6, 64, 64
DI = SSH * SSD
DC = 4
HP = DI // P
SEG = NTOK + DC - 1
M1_TILES = (T + E * (P - 1)) // P
M2_TILES = (2 * T + E * (P - 1)) // P
M1_H, M2_H = 512, 768
WARM_START, WARM_SCORES, WARM_SORTED, WARM_NORM = 8, 12, (7, 7), 14
WEFF = (3, 6, 9, 12)
TILE_BANK = (4, 5, 6, 7, 1)
SUMS = 8
N_CONST = 38
W2 = 2 * HH * NTOK
SEGW = SSH * NTOK


def token_sums(eng, first, src, row, tot, step):
    w = src.rearrange("p y (r x) -> p (y r) x", x=WIN)
    step(eng.tensor_tensor(row.rearrange("p y r x -> p (y r) x"), w[:, :, 0:GRID], w[:, :, 1:WIN], ALU.add))
    r = row.rearrange("p y (b r) x -> p y b (r x)", r=WIN)
    t = tot[:, 0:T].rearrange("p (b n) -> p b n", n=NTOK)
    step(eng.tensor_tensor(t, r[:, 0, :, 0:NTOK], r[:, 0, :, GRID:GRID + NTOK], ALU.add))
    step(eng.tensor_tensor(t, t, r[:, 1, :, 0:NTOK], ALU.add))
    step(eng.tensor_tensor(t, t, r[:, 1, :, GRID:GRID + NTOK], ALU.add))
    for wy in range(2):
        for xh in range(2):
            half = slice(64 * xh, 64 * xh + 64)
            c = src[half, 1 - wy].rearrange("p (b r x) -> p b r x", r=WIN, x=WIN)
            c = c[:, :, wy:wy + GRID, 1 - xh:1 - xh + GRID]
            th = tot[half, 0:T].rearrange("p (b r x) -> p b r x", r=GRID, x=GRID)
            step(eng.tensor_tensor(th, th, c, ALU.add))


def build(nc, A, out):
    with ExitStack() as ctx:
        def sb(name, shape, dt=F32, scope=ctx):
            return scope.enter_context(nc.sbuf_tensor(name, shape, dt))

        ps = ctx.enter_context(nc.psum_tensor("ps", [P, 8, 512], F32))

        def row_of(b, n, parts=P):
            return ps[0:parts, b:b + n, :].rearrange("p b n -> p (b n)")

        def two_halves(b, parts=P):
            return ps[0:parts, b:b + 2, 0:HB]

        def scratch(name, rows, cols, dt):
            return nc.dram_tensor(name, (rows, cols), dt, kind="Internal").ap()

        token_x = [scratch("token_x0", TPAD, D, F32), scratch("token_x1", TPAD, D, F32)]
        token_y = [scratch("token_y0", TPAD + M1_TILES * P, D, BF16),
                   scratch("token_y1", 2 * TPAD + M2_TILES * P, D, F32)]

        ident = sb("ident", [P, P])
        identb = sb("identb", [P, P], BF16)
        ones = sb("ones", [P, P])
        onesb = sb("onesb", [P, P], BF16)
        earlier = sb("earlier", [P, P], BF16)
        head_mask = sb("head_mask", [DH, HH])
        later_blk = sb("later_blk", [P, P])
        upto = sb("upto", [P, NTOK])
        causal = sb("causal", [P, 2, NTOK])
        iota_e = sb("iota_e", [P, E])
        iota_t = sb("iota_t", [1, M2_TILES, E])
        inv_k = sb("inv_k", [P, 1])
        eps_t = sb("eps_t", [P, 1])
        eps2_t = sb("eps2_t", [P, 1])
        root = sb("root", [P, 1])
        magic_t = sb("magic_t", [P, 1])
        neg_magic = sb("neg_magic", [P, 1])
        neg_r = sb("neg_r", [P, P])
        tile_m = sb("tile_m", [P, M2_TILES])
        spare = sb("spare", [P, 2, M2_TILES])
        token_val = sb("token_val", [P, 2, TT, 4], BF16)
        ones8 = sb("ones8", [P, E])
        busy = sb("busy", [P, 512], BF16)

        wqkv = sb("wqkv", [DH, DM, 3 * D])
        wproj = sb("wproj", [DH, DM, D])
        bproj = sb("bproj", [P, D])
        scales = sb("scales", [P, 5])
        tok_b = sb("tok_b", [1, D])
        rw = [sb("rw1", [DH, DM, E]), sb("rw2", [DH, DM, E])]
        rb1 = sb("rb1", [P, E])
        inproj = sb("inproj", [DH, DM, 2 * DI + 2 * SSN + SSH])
        convw = sb("convw", [P, HP + 1, DC])
        convb = sb("convb", [P, HP + 1])
        dskip = sb("dskip", [P, HP])
        dtb = sb("dtb", [P, SSH])
        alog = sb("alog", [P, SSH])
        normw = sb("normw", [P, HP])
        outproj = sb("outproj", [P, HP, D])
        fc1 = sb("fc1", [DH, DM, 2 * DI])
        fc2 = sb("fc2", [P, HP, D])
        ln1 = sb("ln1", [DH, 2, DM])
        ln2 = sb("ln2", [DH, 2, DM])
        arena = ExitStack()
        xp = sb("xp", [P, RING, TPAD], scope=arena)
        arena.close()
        w12 = [sb(f"w12_{i}", [DH, DM, 2 * M2_H]) for i in range(2)]
        w3 = [sb(f"w3_{i}", [P, M2_H // P, D]) for i in range(2)]

        h = sb("h", [P, TT, D])
        hb = sb("hb", [P, TT, D])
        xn = sb("xn", [P, TT, D])
        xt = sb("xt", [DH, DM, TPAD])
        xtp = sb("xtp", [DH, DM, IMGS, 64])
        st6 = sb("st6", [P, TT, 6])
        mv = sb("mv", [P, TT, 2])
        std = sb("std", [P, TT])
        rstd = sb("rstd", [P, TT])
        std2 = sb("std2", [P, TT])
        rstd2 = sb("rstd2", [P, TT])

        logit = sb("logit", [P, TT, E])
        below = sb("below", [P, TT, E])
        ex8 = sb("ex8", [P, TT, E])
        top8 = sb("top8", [P, TT, 8])
        idx8 = sb("idx8", [P, TT, 8], U32)
        idxf = sb("idxf", [P, TT, 2])
        oh = sb("oh", [P, 2, TT, E])
        ohb = sb("ohb", [P, TT, E], BF16)
        tiles_e = sb("tiles_e", [P, E])
        cum_e = sb("cum_e", [P, E])
        base_e = sb("base_e", [P, E])
        rank_b = sb("rank_b", [P, TT, E])
        pick = sb("pick", [P, 2, TT, E])
        slotf = sb("slotf", [P, 2, TT])
        slot_m = sb("slot_m", [P, 2, TT])
        slot_r = sb("slot_r", [P, 2, TT])
        inv = sb("inv", [P, 4, M2_TILES])
        row_f = sb("row_f", [P, 2, M2_TILES])
        src_id = sb("src_id", [P, M2_TILES], I32)
        row_id = sb("row_id", [P, M2_TILES], I32)
        teb = sb("teb", [1, M2_TILES, E])
        tef = sb("tef", [1, M2_TILES])
        te = sb("te", [1, M2_TILES], I32)
        gsum = sb("gsum", [P, TT])
        gate = sb("gate", [P, 2, TT])

        arena = ExitStack()
        xw = sb("xw", [P, CH, 2, NWIN], scope=arena)
        xsq = sb("xsq", [P, CH, 2, NWIN], scope=arena)
        xsum = sb("xsum", [P, 2, NWIN], scope=arena)
        wall = sb("wall", [P, NALL, D], scope=arena)
        weff = sb("weff", [P, NCH, D], scope=arena)
        wug = sb("wug", [P, CH * 2, D], scope=arena)
        gam = sb("gam", [P, NALL], scope=arena)
        bet = sb("bet", [P, NALL], scope=arena)
        row = sb("row", [P, 2, 2, IMGS * WIN, GRID], scope=arena)
        tot = sb("tot", [P, 2, TPAD], scope=arena)
        acc = sb("acc", [P, 3, D], scope=arena)
        s12 = sb("s12", [P, 2, D], scope=arena)
        mom = sb("mom", [P, TT, 2], scope=arena)
        negmu = sb("negmu", [P, TT], scope=arena)
        pstd = sb("pstd", [P, TT], scope=arena)
        prstd = sb("prstd", [P, TT], scope=arena)
        var = sb("var", [P, TT], scope=arena)
        arena.close()

        arena = ExitStack()
        qf = sb("qf", [DH, 4, T], scope=arena)
        qi = sb("qi", [DH, DM, T], scope=arena)
        kc = sb("kc", [DH, DM, T], scope=arena)
        ki = sb("ki", [DH, DM, IMGS, 64], BF16, scope=arena)
        qe = sb("qe", [DH, DM, IMGS, HH, NTOK], BF16, scope=arena)
        vf = sb("vf", [P, PAIRS, D], scope=arena)
        vc = sb("vc", [P, PAIRS, D], scope=arena)
        vi = sb("vi", [P, 2, PAIRS, D], BF16, scope=arena)
        pre = sb("pre", [P, 2, W2], scope=arena)
        at = sb("at", [P, 2, 512], BF16, scope=arena)
        of = sb("of", [P, PAIRS, D], scope=arena)
        oc = sb("oc", [P, PAIRS, D], scope=arena)
        oi = sb("oi", [P, PAIRS, D], BF16, scope=arena)
        ot = sb("ot", [DH, DM, TPAD], scope=arena)
        rsc = sb("rsc", [P, 5], scope=arena)
        c_sc = sb("c_sc", [P, 4], scope=arena)
        arena.close()

        arena = ExitStack()
        at_r = sb("at_r", [P, 2 * TT, P], BF16, scope=arena)
        at_n = sb("at_n", [P, 2 * TT, M2_TILES], BF16, scope=arena)
        val_n = sb("val_n", [P, 2 * TT, 4, M2_TILES], BF16, scope=arena)
        xg = sb("xg", [P, M2_TILES, D], scope=arena)
        xgt = sb("xgt", [DH, DM, M2_TILES * P], scope=arena)
        sg = sb("sg", [P, 2, M2_H // 2], scope=arena)
        ht = sb("ht", [P, 2, M2_H // 2], scope=arena)
        ysb = [sb("ysb0", [P, 2, D], BF16, scope=arena), sb("ysb1", [P, 2, D], scope=arena)]
        yg = [sb("yg0", [P, 1, TT, D], BF16, scope=arena), sb("yg1", [P, 2, TT, D], scope=arena)]
        arena.close()

        arena = ExitStack()
        xn2 = sb("xn2", [P, TT, D], scope=arena)
        xpad = sb("xpad", [P, HP + 1, IMGS, SEG], scope=arena)
        cv = sb("cv", [P, HP + 1, IMGS, NTOK], scope=arena)
        xst = sb("xst", [P, HP, IMGS, 64], scope=arena)
        bt = sb("bt", [SSN, IMGS, 64], scope=arena)
        ct = sb("ct", [SSN, IMGS, 64], scope=arena)
        zs = sb("zs", [P, HP, T], scope=arena)
        dtr = sb("dtr", [SSH, IMGS, 64], scope=arena)
        ssr = sb("ssr", [1, TPAD], scope=arena)
        dtw = sb("dtw", [P, 8, PAIRS, SSH], scope=arena)
        nega = sb("nega", [P, 3, SSH], scope=arena)
        av = sb("av", [P, PAIRS, SSH, NTOK], scope=arena)
        dec = sb("dec", [P, PAIRS, SSH, NTOK], scope=arena)
        gm = sb("gm", [P, PAIRS, 2, NTOK], scope=arena)
        mix = sb("mix", [P, PAIRS, SSH, 2, NTOK], scope=arena)
        dtx = sb("dtx", [P, PAIRS, DI], scope=arena)
        yt = sb("yt", [P, HP, TPAD], scope=arena)
        ysq = sb("ysq", [P, HP, TPAD], scope=arena)
        arena.close()
        x2 = xn2
        ft, sgf = yt, ysq

        S = {n: ctx.enter_context(nc.semaphore(n)) for n in """
            d_gam d_x0 d_x0b d_w0b d_wub d_x1 d_x2 d_w0 d_w1 d_w2 d_wu d_att d_ssm d_tx d_out
            d_xg0 d_xg1 d_xg2 d_xg3 d_xg4 d_w12a d_w12b d_w3a d_w3b d_ya d_yb d_yg d_yg2
            g_const g_pad g_sq a_beta g_wout g_hb g_ssm
            v_c v_rs v_top a_cv a_dtr a_ssr v_wug v_weff v_st v_acc v_h v_bn v_mv v_xn v_xt v_qe v_ki v_vi v_pre v_clip v_oi v_ot
            v_var v_lg v_oh v_te v_gt v_ht v_cv v_u v_one g_mix a_root v_id v_src v_inv v_la g_av v_gm v_mix v_dtx v_ys v_yz
            v_x2 v_fc v_cs
            a_sq a_xp a_s12 a_std a_xt a_qf a_vf a_at a_of a_ot a_ex a_gt a_sg a_y a_cp a_z a_xs a_dt
            a_dec a_ysq a_fc
            p_ch p_st p_ht p_tr p_qk p_v p_sc p_av p_otr p_proj p_lg p_rk p_inv p_gt p_gu p_y p_in p_dt p_g
            p_seg p_xs p_ys p_ssq p_out p_fc p_f2""".split()}
        d_w12 = (S["d_w12a"], S["d_w12b"])
        d_w3 = (S["d_w3a"], S["d_w3b"])
        d_y = (S["d_ya"], S["d_yb"])
        MOE = (dict(n=M1_TILES, hid=M1_H, k=1, w12=A["m1_w12"], w3=A["m1_w3"], before=0),
               dict(n=M2_TILES, hid=M2_H, k=2, w12=A["m2_w12"], w3=A["m2_w3"], before=M1_TILES))
        for r in MOE:
            q = r["n"] // 4
            r["groups"] = [(0, 1), (1, q), (q, 2 * q), (2 * q, 3 * q), (3 * q, 4 * q)]
            r["group_of"] = [i for i, (lo, hi) in enumerate(r["groups"]) for _ in range(lo, hi)]
        N_ATT, N_SSM, N_FIRST = 16 * 7, 16 * 13, 10

        block = ctx.enter_context(nc.Block())

        @block.sync
        def _(sp):
            def load(dst, src, s):
                sp.dma_start(dst, src).then_inc(S[s], 16)

            load(gam[:], A["gam"], "d_gam")
            load(bet[:], A["bet"], "d_gam")
            load(wall[:, NCH:NCH + 2, :], A["w_un"][:, 0:2, :], "d_wu")
            for yh in range(2):
                k = slice(4 * yh, 4 * yh + 4)
                load(wall[:, k, :], A["w_sh"][:, k, :], ("d_w0", "d_w0b")[yh])
                load(xw[:, 0, yh], A["xw"][:, 0, yh], ("d_x0", "d_x0b")[yh])
            load(wall[:, NCH + 2:NALL, :], A["w_un"][:, 2:, :], "d_wub")
            for c in range(1, CH):
                load(wall[:, 8 * c:8 * c + 8, :], A["w_sh"][:, 8 * c:8 * c + 8, :], f"d_w{c}")
                load(xw[:, c], A["xw"][:, c], f"d_x{c}")
            for dst, name in ((wqkv, "wqkv"), (wproj, "wproj"), (bproj, "bproj"), (scales, "scales"),
                              (tok_b, "tok_b"), (rw[0], "rw1"), (rb1, "rb1")):
                load(dst[:], A[name], "d_att")
            for dst, name in ((rw[1], "rw2"), (inproj, "inproj"), (convw, "convw"), (convb, "convb"),
                              (dskip, "dskip"), (dtb, "dtb"), (alog, "alog"), (normw, "normw"),
                              (outproj, "outproj"), (fc1, "fc1"), (fc2, "fc2"), (ln1, "ln1"), (ln2, "ln2")):
                load(dst[:], A[name], "d_ssm")

            def experts_io(m):
                r = MOE[m]
                n, hid, before = r["n"], r["hid"], r["before"]

                def expert(j):
                    return sp.value_load(te[0:1, bass.ds(j, 1)], min_val=0, max_val=E - 1)

                def up_weights(e, b):
                    sp.dma_start(w12[b][:, :, 0:2 * hid],
                                 r["w12"][bass.ds(e, 1)].rearrange("e p m n -> (e p) m n")).then_inc(d_w12[b], 16)

                def down_weights(e, b):
                    sp.dma_start(w3[b][:, 0:hid // P, :],
                                 r["w3"][bass.ds(e, 1)].rearrange("e p c n -> (e p) c n")).then_inc(d_w3[b], 16)

                sp.wait_ge(S["v_xn"], TT * (2 if m == 0 else 6))
                load(token_x[m].rearrange("(t p) d -> p t d", p=P), xn[:], "d_tx")
                sp.wait_ge(S["v_te"], m + 1)
                e = expert(0)
                up_weights(e, 0)
                sp.wait_ge(S["d_xg0"], 16 * (m + 1))
                down_weights(e, 0)
                e = expert(1)
                up_weights(e, 1)
                down_weights(e, 1)
                with sp.Fori(1, n // 2) as i:
                    for b in range(2):
                        e = expert(i * 2 + b)
                        sp.wait_ge(S["p_gu"], i * 4 + (2 * b - 2 + 2 * before))
                        up_weights(e, b)
                        sp.wait_ge(S["p_y"], i * 2 + (b - 1 + before))
                        down_weights(e, b)
                for b in range(2):
                    sp.wait_ge(d_y[b], 8 * (n + before))
                for k in range(r["k"]):
                    y = token_y[m][k * TPAD:(k + 1) * TPAD, :].rearrange("(t p) d -> p t d", p=P)
                    s = ("d_yg", "d_yg2")[k]
                    load(yg[m][:, k, 0:TT - 1, :], y[:, 0:TT - 1], s)
                    load(yg[m][0:LAST, k, TT - 1, :], y[0:LAST, TT - 1], s)

            experts_io(0)
            experts_io(1)
            for t in range(TT):
                rows = P if t < TT - 1 else LAST
                sp.wait_ge(S["v_h"], 5 * TT + t + 1)
                load(out[t * P:t * P + rows, :], h[0:rows, t, :], "d_out")
            sp.wait_ge(S["d_out"], 16 * TT)

        @block.gpsimd
        def _(pool):
            g = nc.gpsimd
            made = [0]

            def const(ins):
                made[0] += 1
                ins.then_inc(S["g_const"], 1)
                pool.wait_ge(S["g_const"], made[0])

            const(g.memset(ones[:], 1.0))
            const(g.memset(inv_k[:], 1.0 / KTOK))
            const(g.memset(eps_t[:], EPS))
            const(g.memset(eps2_t[:], EPS * EPS))
            const(g.memset(magic_t[:], MAGIC))
            const(g.memset(neg_magic[:], -MAGIC))
            const(g.memset(tot[:, :, T:TPAD], 0.0))
            const(g.memset(xp[:, :, T:TPAD], 0.0))
            const(g.memset(busy[:], 0.0))
            const(g.affine_select(out=ident[:], in_=ones[:], compare_op=ALU.is_equal, fill=0.0, base=0,
                                  pattern=[[-1, P]], channel_multiplier=1))
            assert made[0] == N_FIRST
            g.memset(xt[:, :, T:TPAD], 0.0).then_inc(S["g_pad"], 1)
            g.memset(xtp[:, :, :, NTOK:64], 0.0).then_inc(S["g_pad"], 1)

            n_sq = [0]

            def step(ins):
                n_sq[0] += 1
                ins.then_inc(S["g_sq"], 1)
                pool.wait_ge(S["g_sq"], n_sq[0])

            pool.wait_ge(S["a_sq"], 2)
            step(g.tensor_tensor(xsq[:, 0], xsq[:, 0], xsq[:, 1], ALU.add))
            pool.wait_ge(S["a_sq"], 3)
            step(g.tensor_tensor(xsq[:, 0], xsq[:, 0], xsq[:, 2], ALU.add))
            token_sums(g, 0, xsq[:, 0], row[:, 1], tot[:, 1], step)
            assert n_sq[0] == SUMS + 2

            const(g.memset(onesb[:], 1.0))
            const(g.memset(ones8[:], 1.0))
            const(g.memset(later_blk[:], 0.0))
            const(g.memset(causal[:], 0.0))
            const(g.affine_select(out=identb[:], in_=ones[:], compare_op=ALU.is_equal, fill=0.0, base=0,
                                  pattern=[[-1, P]], channel_multiplier=1))
            const(g.affine_select(out=earlier[:], in_=ones[:], compare_op=ALU.is_gt, fill=0.0, base=0,
                                  pattern=[[1, P]], channel_multiplier=-1))
            const(g.affine_select(out=head_mask[:], in_=ones[0:DH, 0:HH], compare_op=ALU.is_ge, fill=0.0,
                                  base=0, pattern=[[-HD, HH]], channel_multiplier=1))
            const(g.affine_select(out=head_mask[:], in_=head_mask[:], compare_op=ALU.is_ge, fill=0.0,
                                  base=HD - 1, pattern=[[HD, HH]], channel_multiplier=-1))
            for i in range(2):
                r = slice(64 * i, 64 * i + 64)
                const(g.affine_select(out=later_blk[r, r], in_=ones[r, 0:64], compare_op=ALU.is_gt, fill=0.0,
                                      base=0, pattern=[[-1, 64]], channel_multiplier=1))
                const(g.affine_select(out=later_blk[r, r], in_=later_blk[r, r], compare_op=ALU.is_ge, fill=0.0,
                                      base=NTOK - 1, pattern=[[0, 64]], channel_multiplier=-1))
                const(g.affine_select(out=upto[r, :], in_=ones[r, 0:NTOK], compare_op=ALU.is_ge, fill=0.0,
                                      base=0, pattern=[[1, NTOK]], channel_multiplier=-1))
                const(g.affine_select(out=causal[r, i, :], in_=ones[r, 0:NTOK], compare_op=ALU.is_ge, fill=0.0,
                                      base=0, pattern=[[1, NTOK]], channel_multiplier=-1))
            const(g.iota(iota_e[:], pattern=[[1, E]], base=0, channel_multiplier=0,
                         allow_small_or_imprecise_dtypes=True))
            const(g.iota(iota_t[:], pattern=[[1, M2_TILES], [0, E]], base=0, channel_multiplier=0,
                         allow_small_or_imprecise_dtypes=True))
            def iota(out, pattern, base=0, channel_multiplier=0):
                const(g.iota(out, pattern=pattern, base=base, channel_multiplier=channel_multiplier,
                             allow_small_or_imprecise_dtypes=True))

            iota(neg_r[:], [[-1, P]])
            const(g.tensor_scalar(neg_r[:], neg_r[:], 1.0 / P, None, ALU.mult))
            iota(tile_m[:], [[1, M2_TILES]])
            const(g.tensor_scalar(tile_m[:], tile_m[:], MAGIC, None, ALU.add))
            for m in range(2):
                iota(spare[:, m], [[P, M2_TILES]], base=(m + 1) * TPAD, channel_multiplier=1)
            tv = token_val[:].rearrange("p k t c -> p c k t")
            iota(tv[:, 0], [[0, 2], [0, TT]], channel_multiplier=1)
            iota(tv[:, 1], [[0, 2], [1, TT]])
            iota(tv[:, 2], [[1, 2], [0, TT]])
            const(g.memset(tv[:, 3], 1.0))
            assert made[0] == N_CONST

            pool.wait_ge(S["v_h"], TT)
            g.memset(ki[:, :, :, NTOK:64], 0.0).then_inc(S["g_pad"], 1)
            g.memset(vi[:], 0.0).then_inc(S["g_pad"], 1)
            g.memset(at[:, :, W2:512], 0.0).then_inc(S["g_pad"], 1)
            g.memset(ot[:, :, T:TPAD], 0.0).then_inc(S["g_pad"], 1)
            pool.wait_ge(S["d_att"], N_ATT)
            g.tensor_tensor(hb[:], h[:], bproj[:].unsqueeze(1).broadcast_to([P, TT, D]), ALU.add)\
                .then_inc(S["g_hb"], 1)
            pool.wait_ge(S["d_ssm"], N_SSM)
            g.tensor_tensor(outproj[:], outproj[:], normw[:].unsqueeze(2).broadcast_to([P, HP, D]), ALU.mult)\
                .then_inc(S["g_wout"], 1)

            def experts_io(m):
                r = MOE[m]
                n, before = r["n"], r["before"]
                pool.wait_ge(S["v_src"], m + 1)
                pool.wait_ge(S["d_tx"], 16 * (m + 1))
                for j in range(n):
                    g.indirect_dma_start(
                        xg[:, j, :], None, token_x[m],
                        bass.IndirectOffsetOnAxis(ap=src_id[:, j:j + 1], axis=0))\
                        .then_inc(S[f"d_xg{r['group_of'][j]}"], 16)
                pool.wait_ge(S["v_id"], m + 1)
                for j in range(n):
                    pool.wait_ge(S["a_y"], j + 1 + before)
                    g.indirect_dma_start(
                        token_y[m], bass.IndirectOffsetOnAxis(ap=row_id[:, j:j + 1], axis=0),
                        ysb[m][:, j % 2, :], None).then_inc(d_y[j % 2], 16)

            experts_io(0)
            pool.wait_ge(S["v_h"], 3 * TT)
            g.memset(xpad[:, :, :, 0:DC - 1], 0.0).then_inc(S["g_ssm"], 1)
            g.memset(xst[:, :, :, NTOK:64], 0.0).then_inc(S["g_ssm"], 1)
            g.memset(bt[:, :, NTOK:64], 0.0).then_inc(S["g_ssm"], 1)
            g.memset(yt[:, :, T:TPAD], 0.0).then_inc(S["g_ssm"], 1)
            g.memset(dtr[:, :, NTOK:64], 0.0).then_inc(S["g_ssm"], 1)
            g.memset(ssr[:, T:TPAD], 0.0).then_inc(S["g_ssm"], 1)
            pool.wait_ge(S["v_la"], 1)
            g.tensor_tensor(av[:].rearrange("p j h n -> p (j h) n"),
                            dtw[:, 1].rearrange("p j h -> p (j h)").unsqueeze(2)
                            .broadcast_to([P, PAIRS * SSH, NTOK]),
                            upto[:].unsqueeze(1).broadcast_to([P, PAIRS * SSH, NTOK]), ALU.mult)\
                .then_inc(S["g_av"], 1)
            pool.wait_ge(S["v_gm"], 1)
            for j in range(1, PAIRS, 2):
                pool.wait_ge(S["a_dec"], j // 2 + 1)
                g.tensor_tensor(mix[:, j], dec[:, j].unsqueeze(2).broadcast_to([P, SSH, 2, NTOK]),
                                gm[:, j].unsqueeze(1).broadcast_to([P, SSH, 2, NTOK]), ALU.mult)\
                    .then_inc(S["g_mix"], 1)
            pool.wait_ge(S["v_x2"], TT)
            g.tensor_tensor(hb[:], h[:], x2[:], ALU.add).then_inc(S["g_hb"], 1)
            experts_io(1)

        @block.scalar
        def _(act):
            a = nc.scalar
            for c in range(CH):
                act.wait_ge(S[f"d_x{c}"], 16)
                for k in range(8):
                    if (c, k) == (0, 4):
                        act.wait_ge(S["d_x0b"], 16)
                    wy, wx = k % 4 // 2, k % 2
                    n = 8 * c + k
                    if n >= RING:
                        act.wait_ge(S["p_ch"], n - RING + 1)
                    img = xw[:, c, k // 4].rearrange("p (b r x) -> p b r x", r=WIN, x=WIN)
                    a.copy(xp[:, n % RING, 0:T].rearrange("p (b r x) -> p b r x", r=GRID, x=GRID),
                           img[:, :, wy:wy + GRID, wx:wx + GRID]).then_inc(S["a_xp"], 1)
                    for sq, place in enumerate((4, 6, 9)):
                        if n == place:
                            act.wait_ge(S[f"d_x{sq}"], 16)
                            a.activation(xsq[:, sq], xw[:, sq], ACT.Square).then_inc(S["a_sq"], 1)
                    act.wait_ge(S["d_gam"], 32)
                    act.wait_ge(S["v_weff"], WEFF[n // 4 if n < 8 else c + 1] - 2)
                    a.activation(wall[:, n, :], wall[:, n, :], ACT.Copy, scale=bet[:, n:n + 1])\
                        .then_inc(S["a_beta"], 1)
            act.wait_ge(S["v_wug"], 2)
            for n in range(NCH, NALL):
                a.activation(wall[:, n, :], wall[:, n, :], ACT.Copy, scale=bet[:, n:n + 1])\
                    .then_inc(S["a_beta"], 1)
            act.wait_ge(S["v_var"], 1)
            a.activation(pstd[:], var[:], ACT.Sqrt, bias=eps_t[:]).then_inc(S["a_std"], 1)
            act.wait_ge(S["p_st"], 3)
            a.copy(s12[:].rearrange("p s d -> p (s d)"), ps[:, 3, 0:2 * D]).then_inc(S["a_s12"], 1)

            def deviations(i, twice=False):
                for t in range(TT):
                    act.wait_ge(S["v_mv"], TT * (i - 1) + t + 1)
                    a.activation(std[:, t:t + 1], mv[:, t, 1:2], ACT.Sqrt,
                                 bias=eps2_t[:] if twice else eps_t[:], scale=1.0 + EPS if twice else 1.0)\
                        .then_inc(S["a_std"], 1)

            def transposed(i, padded=False, ln=None):
                act.wait_ge(S["p_tr"], 2 * i - 1)
                act.wait_ge(S["g_pad"], 2)
                src = row_of(0, 2, DH)[:, 0:T]
                dst = xt[:, 0, 0:T]
                if padded:
                    src = src.rearrange("p (b n) -> p b n", n=NTOK)
                    dst = xtp[:, 0, :, 0:NTOK]
                if ln is None:
                    a.copy(dst, src).then_inc(S["a_xt"], 1)
                else:
                    act.wait_ge(S["d_ssm"], N_SSM)
                    a.activation(dst, src, ACT.Identity, bias=ln[:, 1, 0:1],
                                 scale=ln[:, 0, 0:1]).then_inc(S["a_xt"], 1)

            deviations(1)
            transposed(1, padded=True)
            act.wait_ge(S["v_cs"], 3)
            for r in range(4):
                if r == 2:
                    act.wait_ge(S["p_v"], 1)
                    a.activation(vf[:].rearrange("p (b j) d -> p b (j d)", j=2), ps[:, 0:4, 0:2 * D], ACT.Identity,
                                 bias=magic_t[:], scale=rsc[:, 2:3]).then_inc(S["a_vf"], 1)
                act.wait_ge(S["p_qk"], r + 1)
                a.activation(qf[:, r, :].rearrange("p (b n) -> p b n", b=2), two_halves(4 + 2 * (r % 2), DH),
                             ACT.Identity,
                             bias=magic_t[0:DH, :], scale=rsc[0:DH, r // 2:r // 2 + 1]).then_inc(S["a_qf"], 1)
            act.wait_ge(S["g_pad"], 6)
            for j in range(PAIRS):
                act.wait_ge(S["v_clip"], j + 1)
                if j >= 2:
                    act.wait_ge(S["p_av"], j - 1)
                a.activation(at[:, j % 2, 0:W2], pre[:, j % 2, :], ACT.Relu,
                             bias=neg_magic[:]).then_inc(S["a_at"], 1)
            for q in range(4):
                act.wait_ge(S["p_av"], 2 * q + 2)
                a.activation(of[:, 2 * q:2 * q + 2, :].rearrange("p j d -> p (j d)"), ps[:, q, 0:2 * D],
                             ACT.Identity, bias=magic_t[:], scale=c_sc[:, 1:2]).then_inc(S["a_of"], 1)
            act.wait_ge(S["p_otr"], 1)
            a.copy(ot[:, 0, 0:T].rearrange("p (b n) -> p b n", n=NTOK),
                   ps[0:DH, 4, :].bitcast(BF16).rearrange("p (b n) -> p b n", n=64)[:, :, 0:NTOK])\
                .then_inc(S["a_ot"], 1)

            def experts(m):
                r = MOE[m]
                n, half, before = r["n"], r["hid"] // 2, r["before"]
                deviations(2 if m == 0 else 5)
                transposed(2 if m == 0 else 5)
                act.wait_ge(S["v_lg"], m + 1)
                s = slice(0, E) if m == 0 else slice(0, 1)
                a.activation(ex8[:, :, s], below[:, :, s], ACT.Exp).then_inc(S["a_ex"], 1)

                def gathered(i):
                    lo, hi = r["groups"][i]
                    act.wait_ge(S["p_gt"], 10 * m + 2 * i + 1)
                    a.copy(xgt[:, 0, lo * P:hi * P], ps[0:DH, 6, 0:(hi - lo) * P]).then_inc(S["a_gt"], 1)

                def silu(j, s):
                    act.wait_ge(S["p_gu"], j * 2 + (s + 1 + 2 * before))
                    a.activation(sg[:, s, 0:half], ps[:, 2 * s, 0:half], ACT.Silu).then_inc(S["a_sg"], 1)

                def result(j, b, stored=None):
                    act.wait_ge(S["p_y"], j + (1 + before))
                    if stored is not None:
                        act.wait_ge(d_y[b], stored * 16 + 8 * before)
                    a.copy(ysb[m][:, b, :], ps[:, 4 + b, 0:D]).then_inc(S["a_y"], 1)

                gathered(0)
                silu(0, 0)
                silu(0, 1)
                gathered(1)
                for j in (1, 2):
                    silu(j, 0)
                    if j == 2:
                        gathered(3)
                    result(j - 1, 1 - j % 2)
                    silu(j, 1)
                    gathered(2 * j)
                with act.Fori(2, n // 2) as i:
                    for b in (1, 0):
                        j = i * 2 - b
                        silu(j, 0)
                        result(j - 1, 1 - b, i - 1)
                        silu(j, 1)
                silu(n - 1, 0)
                result(n - 2, 0, n // 2 - 1)
                silu(n - 1, 1)
                result(n - 1, 1, n // 2 - 1)

            experts(0)

            deviations(3, twice=True)
            a.activation(std2[:], mv[:, :, 1], ACT.Sqrt, bias=eps_t[:]).then_inc(S["a_std"], 1)
            transposed(3, padded=True, ln=ln1)
            act.wait_ge(S["p_dt"], 1)
            act.wait_ge(S["g_ssm"], 5)
            a.copy(dtr[:, :, 0:NTOK].rearrange("p (b i) n -> p b i n", b=2),
                   two_halves(6, SSH).rearrange("p b (i n) -> p b i n", n=NTOK)).then_inc(S["a_dtr"], 1)
            act.wait_ge(S["v_u"], 1)
            a.activation(nega[:, 0], nega[:, 2], ACT.Exp).then_inc(S["a_dt"], 1)
            act.wait_ge(S["v_u"], 2)
            a.activation(dtw[:, 2], dtw[:, 1], ACT.Exp, scale=-1.0).then_inc(S["a_dt"], 1)
            act.wait_ge(S["v_one"], 1)
            a.activation(dtw[:, 4], dtw[:, 3], ACT.Ln).then_inc(S["a_dt"], 1)
            act.wait_ge(S["g_ssm"], 1)
            for s, r in enumerate((3, 0, 1, 2)):
                act.wait_ge(S["p_in"], s + 1)
                for b in range(2):
                    a.copy(xpad[:, r, 8 * b:8 * b + 8, DC - 1:SEG],
                           ps[:, 2 * s + b, 0:HB].rearrange("p (i n) -> p i n", n=NTOK))\
                        .then_inc(S["a_cp"], 1)
                act.wait_ge(S["a_cp"], 2 * s + 2)
                a.activation(cv[:, r], xpad[:, r, :, 0:NTOK], ACT.Identity, bias=convb[:, r:r + 1],
                             scale=convw[:, r, 0:1]).then_inc(S["a_cv"], 1)
            for r in range(HP):
                act.wait_ge(S["p_in"], 5 + r)
                a.activation(zs[:, r, :].rearrange("p (b n) -> p b n", b=2), two_halves(2 * r),
                             ACT.Silu).then_inc(S["a_z"], 1)
            act.wait_ge(S["v_cv"], DC - 1)
            act.wait_ge(S["g_ssm"], 3)
            a.activation(bt[:, :, 0:NTOK], cv[0:SSN, HP], ACT.Silu).then_inc(S["a_xs"], 1)
            a.activation(ct[:, :, 0:NTOK], cv[SSN:P, HP], ACT.Silu).then_inc(S["a_xs"], 1)
            for r in range(HP):
                act.wait_ge(S["v_cv"], (DC - 1) * (r + 2))
                a.activation(xst[:, r, :, 0:NTOK], cv[:, r], ACT.Silu).then_inc(S["a_xs"], 1)
            for q in range(4):
                act.wait_ge(S["p_seg"], q + 1)
                a.activation(dec[:, 2 * q:2 * q + 2].rearrange("p j h n -> p (j h n)"),
                             ps[:, q, 0:2 * SEGW], ACT.Exp).then_inc(S["a_dec"], 1)
            for r in range(HP):
                act.wait_ge(S["v_yz"], r + 1)
                a.activation(ysq[:, r, 0:T], yt[:, r, 0:T], ACT.Square).then_inc(S["a_ysq"], 1)
            a.activation(root[:], eps_t[:], ACT.Sqrt).then_inc(S["a_root"], 1)
            act.wait_ge(S["p_ssq"], 1)
            a.copy(ssr[:, 0:T].rearrange("p (b n) -> p b n", b=2), two_halves(6, 1)).then_inc(S["a_ssr"], 1)
            act.wait_ge(S["p_ssq"], 2)
            a.activation(std2[:], ps[:, 3, 0:TT], ACT.Sqrt, bias=eps_t[:], scale=1.0 / DI)\
                .then_inc(S["a_std"], 1)
            deviations(4)
            transposed(4, ln=ln2)
            for r in range(HP):
                act.wait_ge(S["p_fc"], 2 * r + 2)
                a.activation(sgf[:, r, 0:T].rearrange("p (b n) -> p b n", b=2),
                             two_halves(4 * (r % 2) + 2), ACT.Silu).then_inc(S["a_fc"], 1)
            experts(1)

        @block.vector
        def _(dve):
            v = nc.vector
            chain = [0]

            def link(ins):
                chain[0] += 1
                ins.then_inc(S["v_c"], 1)
                dve.wait_ge(S["v_c"], chain[0])

            dve.wait_ge(S["d_gam"], 32)
            n_weff = [0]

            def chunks(c, lo, hi):
                k = slice(8 * c + lo, 8 * c + hi)
                v.tensor_tensor(weff[:, k, :], wall[:, k, :],
                                gam[:, k].unsqueeze(2).broadcast_to([P, hi - lo, D]), ALU.mult)\
                    .then_inc(S["v_weff"], 1)
                n_weff[0] += 1
                dve.wait_ge(S["v_weff"], n_weff[0])
                for xh in range(2):
                    half = slice(64 * xh, 64 * xh + 64)
                    centre = [n for n in (3 - xh, 5 - xh) if lo <= n < hi]
                    w = weff[half, 8 * c + centre[0]:8 * c + centre[-1] + 1:2, :]
                    u = 2 * c + (centre[0] - 3 + xh) // 2
                    v.tensor_tensor(w, w, wug[half, u:u + len(centre), :], ALU.add).then_inc(S["v_weff"], 1)
                    n_weff[0] += 1

            for first, last, arrived in ((0, 2, "d_wu"), (2, 2 * CH, "d_wub")):
                dve.wait_ge(S[arrived], 16)
                k = slice(NCH + first, NCH + last)
                v.tensor_tensor(wug[:, first:last, :], wall[:, k, :],
                                gam[:, k].unsqueeze(2).broadcast_to([P, last - first, D]), ALU.mult)\
                    .then_inc(S["v_wug"], 1)
                dve.wait_ge(S["v_wug"], 1 if first == 0 else 2)
                if first == 0:
                    for yh in range(2):
                        dve.wait_ge(S[("d_w0", "d_w0b")[yh]], 16)
                        chunks(0, 4 * yh, 4 * yh + 4)
            for c in range(1, CH):
                dve.wait_ge(S[f"d_w{c}"], 16)
                chunks(c, 0, 8)
            assert n_weff[0] == WEFF[-1]
            n_st = [0]

            def step(ins):
                n_st[0] += 1
                ins.then_inc(S["v_st"], 1)
                dve.wait_ge(S["v_st"], n_st[0])

            for x in ("d_x0", "d_x0b", "d_x1", "d_x2"):
                dve.wait_ge(S[x], 16)
            dve.wait_ge(S["g_const"], N_FIRST)
            step(v.tensor_tensor(xsum[:], xw[:, 0], xw[:, 1], ALU.add))
            step(v.tensor_tensor(xsum[:], xsum[:], xw[:, 2], ALU.add))
            token_sums(v, 0, xsum[:], row[:, 0], tot[:, 0], step)
            assert n_st[0] == SUMS + 2
            dve.wait_ge(S["v_weff"], WEFF[-1])
            v.tensor_reduce(acc[:, 0, :], weff[:].rearrange("p c d -> p d c"), AX.X, ALU.add)\
                .then_inc(S["v_acc"], 1)
            for i, part in enumerate((slice(0, 16), slice(16, NALL))):
                dve.wait_ge(S["a_beta"], part.stop)
                v.tensor_reduce(acc[:, 1 + i, :], wall[:, part].rearrange("p c d -> p d c"), AX.X, ALU.add)\
                    .then_inc(S["v_acc"], 1)
            dve.wait_ge(S["v_acc"], 3)
            v.tensor_tensor(acc[:, 1, :], acc[:, 1, :], acc[:, 2, :], ALU.add).then_inc(S["v_acc"], 1)
            dve.wait_ge(S["v_acc"], 4)
            dve.wait_ge(S["d_att"], N_ATT)
            v.tensor_tensor(acc[0:1, 1, :], acc[0:1, 1, :], tok_b[:], ALU.add).then_inc(S["v_acc"], 1)
            dve.wait_ge(S["p_st"], 1)
            link(v.tensor_copy(mom[:].rearrange("p t s -> p (t s)"), ps[:, 2, 0:2 * TT]))
            link(v.tensor_scalar(negmu[:], mom[:, :, 0], -1.0, None, ALU.mult))
            link(v.tensor_tensor(var[:], negmu[:], negmu[:], ALU.mult))
            link(v.tensor_tensor(var[:], mom[:, :, 1], var[:], ALU.subtract))
            v.tensor_scalar(var[:], var[:], 0.0, None, ALU.max).then_inc(S["v_var"], 1)
            dve.wait_ge(S["a_std"], 1)
            link(v.reciprocal(prstd[:], pstd[:]))
            dve.wait_ge(S["a_s12"], 1)
            def embedded(t):
                dve.wait_ge(S["p_ht"], t + 1)
                link(v.scalar_tensor_tensor(out=h[:, t, :], in0=s12[:, 0, :], scalar=negmu[:, t:t + 1],
                                            in1=ps[:, TILE_BANK[t], 0:D], op0=ALU.mult, op1=ALU.add))
                v.scalar_tensor_tensor(out=h[:, t, :], in0=h[:, t, :], scalar=prstd[:, t:t + 1],
                                       in1=s12[:, 1, :], op0=ALU.mult, op1=ALU.add).then_inc(S["v_h"], 1)


            def statistics(i, t, src, between=None):
                v.bn_stats(st6[:, t, :], src[:, t, :]).then_inc(S["v_bn"], 1)
                if between is not None:
                    between()
                dve.wait_ge(S["v_bn"], TT * (i - 1) + t + 1)
                v.bn_aggr(mv[:, t, :], st6[:, t, :]).then_inc(S["v_mv"], 1)

            def layer_norm(i, tile, src, ready, base, stds, dst=xn):
                n_r = TT * (i - 1)

                def reciprocal(t):
                    dve.wait_ge(S["a_std"], stds + t + 1)
                    v.reciprocal(rstd[:, t:t + 1], std[:, t:t + 1]).then_inc(S["v_rs"], 1)

                def normalised(t):
                    dve.wait_ge(S["v_rs"], n_r + t + 1)
                    v.tensor_scalar(dst[:, t, :], src[:, t, :], mv[:, t, 0:1], rstd[:, t:t + 1],
                                    ALU.subtract, ALU.mult).then_inc(S["v_xn"], 1)

                for t in range(TT):
                    tile(t)
                    if t > 0:
                        reciprocal(t - 1)
                    dve.wait_ge(S[ready], base + t + 1)
                    statistics(i, t, src, None if t == 0 else lambda: normalised(t - 1))
                reciprocal(TT - 1)
                normalised(TT - 1)

            def transposed(i, padded=False, ln=None):
                dve.wait_ge(S["p_tr"], 2 * i)
                dve.wait_ge(S["g_pad"], 2)
                src = row_of(2, 2, DH)[:, 0:T]
                dst = xt[:, 1, 0:T]
                if padded:
                    src = src.rearrange("p (b n) -> p b n", n=NTOK)
                    dst = xtp[:, 1, :, 0:NTOK]
                if ln is None:
                    v.tensor_copy(dst, src).then_inc(S["v_xt"], 1)
                else:
                    dve.wait_ge(S["d_ssm"], N_SSM)
                    v.tensor_scalar(dst, src, ln[:, 0, 1:2], ln[:, 1, 1:2], ALU.mult, ALU.add)\
                        .then_inc(S["v_xt"], 1)

            layer_norm(1, embedded, h, "v_h", 0, 1)
            transposed(1, padded=True)
            v.reciprocal(rsc[:], scales[:]).then_inc(S["v_cs"], 1)
            link(v.tensor_tensor(c_sc[:, 2:3], scales[:, 0:1], scales[:, 1:2], ALU.mult))
            v.tensor_scalar(c_sc[:, 0:1], c_sc[:, 2:3], float(HD) ** -0.5 / NTOK, None, ALU.mult)\
                .then_inc(S["v_cs"], 1)
            link(v.tensor_tensor(c_sc[:, 3:4], scales[:, 3:4], scales[:, 2:3], ALU.mult))
            dve.wait_ge(S["v_cs"], 1)
            v.tensor_tensor(c_sc[:, 1:2], c_sc[:, 3:4], rsc[:, 4:5], ALU.mult).then_inc(S["v_cs"], 1)
            dve.wait_ge(S["g_const"], N_CONST)
            for m in range(DM):
                dve.wait_ge(S["a_qf"], m + 1)
                link(v.tensor_scalar(qi[:, m, :], qf[:, m, :], MAGIC, QLO, ALU.subtract, ALU.max))
                for hh in range(HH):
                    v.tensor_scalar(qe[:, m, :, hh, :], qi[:, m, :].rearrange("p (b n) -> p b n", n=NTOK),
                                    QHI, head_mask[:, hh:hh + 1], ALU.min, ALU.mult).then_inc(S["v_qe"], 1)
            dve.wait_ge(S["a_vf"], 1)
            link(v.tensor_scalar(vc[:], vf[:], MAGIC, QLO, ALU.subtract, ALU.max))
            dve.wait_ge(S["g_pad"], 4)
            for i in range(2):
                r = slice(64 * i, 64 * i + 64)
                v.tensor_scalar(vi[r, i], vc[r], QHI, None, ALU.min).then_inc(S["v_vi"], 1)
            dve.wait_ge(S["g_pad"], 6)
            for m in range(DM):
                dve.wait_ge(S["a_qf"], m + 3)
                link(v.tensor_scalar(kc[:, m, :], qf[:, 2 + m, :], MAGIC, QLO, ALU.subtract, ALU.max))
                v.tensor_scalar(ki[:, m, :, 0:NTOK], kc[:, m, :].rearrange("p (b n) -> p b n", n=NTOK),
                                QHI, None, ALU.min).then_inc(S["v_ki"], 1)

            dve.wait_ge(S["v_cs"], 3)
            for j in range(PAIRS):
                dve.wait_ge(S["p_sc"], j + 1)
                if j >= 2:
                    dve.wait_ge(S["a_at"], j - 1)
                v.tensor_scalar(pre[:, j % 2, :], ps[:, 4 + j % 3, 0:W2], c_sc[:, 0:1], rsc[:, 3:4],
                                ALU.mult, ALU.mult).then_inc(S["v_pre"], 1)
                dve.wait_ge(S["v_pre"], j + 1)
                v.tensor_scalar(pre[:, j % 2, :], pre[:, j % 2, :], AHI, MAGIC, ALU.min, ALU.add)\
                    .then_inc(S["v_clip"], 1)
            for q in range(4):
                dve.wait_ge(S["a_of"], q + 1)
                j2 = slice(2 * q, 2 * q + 2)
                link(v.tensor_scalar(oc[:, j2], of[:, j2], MAGIC, QLO, ALU.subtract, ALU.max))
                v.tensor_scalar(oi[:, j2], oc[:, j2], QHI, None, ALU.min).then_inc(S["v_oi"], 1)
            dve.wait_ge(S["p_otr"], 2)
            v.tensor_copy(ot[:, 1, 0:T].rearrange("p (b n) -> p b n", n=NTOK),
                          ps[0:DH, 5, :].bitcast(BF16).rearrange("p (b n) -> p b n", n=64)[:, :, 0:NTOK])\
                .then_inc(S["v_ot"], 1)
            dve.wait_ge(S["g_hb"], 1)

            def attended(t):
                dve.wait_ge(S["p_proj"], t + 1)
                v.scalar_tensor_tensor(out=h[:, t, :], in0=ps[:, TILE_BANK[t], 0:D], scalar=scales[:, 4:5],
                                       in1=hb[:, t, :], op0=ALU.mult, op1=ALU.add).then_inc(S["v_h"], 1)

            def experts(m, tile):
                r = MOE[m]
                n, half, before, K = r["n"], r["hid"] // 2, r["before"], r["k"]
                i_ln = 2 if m == 0 else 5
                layer_norm(i_ln, tile, h, "v_h", TT * (1 if m == 0 else 3),
                           TT + 1 if m == 0 else 4 * TT + 3)
                transposed(i_ln)
                dve.wait_ge(S["p_lg"], m + 1)
                lg = ps[:, 6, 0:TT * E].rearrange("p (t e) -> p t e", e=E)
                if m == 0:
                    link(v.tensor_tensor(logit[:], lg, rb1[:].unsqueeze(1).broadcast_to([P, TT, E]), ALU.add))
                else:
                    link(v.tensor_copy(logit[:], lg))
                for t in range(TT):
                    v.max(top8[:, t, :], logit[:, t, :]).then_inc(S["v_top"], 1)
                for t in range(TT):
                    dve.wait_ge(S["v_top"], TT * 2 * m + t + 1)
                    v.max_index(idx8[:, t, :], top8[:, t, :], logit[:, t, :]).then_inc(S["v_top"], 1)
                dve.wait_ge(S["v_top"], TT * (2 * m + 2))
                link(v.tensor_copy(idxf[:], idx8[:, :, 0:2]))
                link(v.tensor_tensor(oh[:, 0:K], idxf[:].rearrange("p t k -> p k t")[:, 0:K].unsqueeze(3)
                                     .broadcast_to([P, K, TT, E]),
                                     iota_e[:].unsqueeze(1).unsqueeze(1).broadcast_to([P, K, TT, E]),
                                     ALU.is_equal))
                if K == 1:
                    v.tensor_copy(ohb[:], oh[:, 0]).then_inc(S["v_oh"], 1)
                    v.tensor_tensor(below[:], logit[:], top8[:, :, 0:1].broadcast_to([P, TT, E]),
                                    ALU.subtract).then_inc(S["v_lg"], 1)
                else:
                    v.tensor_tensor(ohb[:], oh[:, 0], oh[:, 1], ALU.add).then_inc(S["v_oh"], 1)
                    v.tensor_tensor(below[:, :, 0:1], top8[:, :, 1:2], top8[:, :, 0:1],
                                    ALU.subtract).then_inc(S["v_lg"], 1)
                dve.wait_ge(S["p_rk"], m + 1)
                link(v.tensor_scalar(tiles_e[:], ps[:, 7, TT * E:TT * E + E], (P - 1) / 2, 1.0 / P,
                                     ALU.add, ALU.mult))
                link(v.tensor_scalar(tiles_e[:], tiles_e[:], MAGIC, MAGIC, ALU.add, ALU.subtract))
                link(v.tensor_tensor_scan(cum_e[:], ones8[:], tiles_e[:], 0.0, ALU.mult, ALU.add))
                link(v.tensor_tensor(teb[:, 0:n, :], cum_e[0:1, :].unsqueeze(1).broadcast_to([1, n, E]),
                                     iota_t[:, 0:n, :], ALU.is_le))
                link(v.tensor_reduce(tef[:, 0:n], teb[:, 0:n, :], AX.X, ALU.add))
                v.tensor_scalar(te[:, 0:n], tef[:, 0:n], float(E - 1), None, ALU.min).then_inc(S["v_te"], 1)
                link(v.tensor_tensor(base_e[:], cum_e[:], tiles_e[:], ALU.subtract))
                link(v.scalar_tensor_tensor(out=rank_b[:],
                                            in0=ps[:, 7, 0:TT * E].rearrange("p (t e) -> p t e", e=E),
                                            scalar=1.0 / P, in1=base_e[:].unsqueeze(1).broadcast_to([P, TT, E]),
                                            op0=ALU.mult, op1=ALU.add))
                link(v.tensor_tensor(pick[:, 0:K], rank_b[:].unsqueeze(1).broadcast_to([P, K, TT, E]),
                                     oh[:, 0:K], ALU.mult))
                link(v.tensor_reduce(slotf[:, 0:K], pick[:, 0:K], AX.X, ALU.add))
                link(v.tensor_scalar(slot_m[:, 0:K], slotf[:, 0:K], -(P - 1) / (2 * P), MAGIC, ALU.add, ALU.add))
                link(v.scalar_tensor_tensor(out=slot_r[:, 0:K], in0=slot_m[:, 0:K], scalar=MAGIC,
                                            in1=slotf[:, 0:K], op0=ALU.subtract, op1=ALU.subtract))
                kt = K * TT
                link(v.tensor_tensor(at_n[:, 0:kt, 0:n], slot_m[:, 0:K].rearrange("p k t -> p (k t)").unsqueeze(2)
                                     .broadcast_to([P, kt, n]),
                                     tile_m[:, 0:n].unsqueeze(1).broadcast_to([P, kt, n]), ALU.is_equal))
                link(v.tensor_tensor(val_n[:, 0:kt, :, 0:n], at_n[:, 0:kt, 0:n].unsqueeze(2)
                                     .broadcast_to([P, kt, 4, n]),
                                     token_val[:, 0:K].rearrange("p k t c -> p (k t) c").unsqueeze(3)
                                     .broadcast_to([P, kt, 4, n]), ALU.mult))
                v.tensor_tensor(at_r[:, 0:kt, :], slot_r[:, 0:K].rearrange("p k t -> p (k t)").unsqueeze(2)
                                .broadcast_to([P, kt, P]),
                                neg_r[:].unsqueeze(1).broadcast_to([P, kt, P]), ALU.is_equal)\
                    .then_inc(S["v_inv"], 1)
                dve.wait_ge(S["p_inv"], m + 1)
                link(v.tensor_copy(inv[:, :, 0:n], ps[:, 5, 0:4 * n].rearrange("p (c n) -> p c n", n=n)))
                v.scalar_tensor_tensor(out=src_id[:, 0:n], in0=inv[:, 1, 0:n], scalar=float(P),
                                       in1=inv[:, 0, 0:n], op0=ALU.mult, op1=ALU.add).then_inc(S["v_src"], 1)
                dve.wait_ge(S["a_ex"], m + 1)
                if K == 1:
                    link(v.tensor_reduce(gsum[:], ex8[:], AX.X, ALU.add))
                    link(v.reciprocal(gate[:, 0], gsum[:]))
                else:
                    link(v.tensor_scalar(gsum[:], ex8[:, :, 0], 1.0, None, ALU.add))
                    link(v.reciprocal(gate[:, 0], gsum[:]))
                    link(v.tensor_tensor(gate[:, 1], gate[:, 0], ex8[:, :, 0], ALU.mult))
                link(v.scalar_tensor_tensor(out=row_f[:, 0, 0:n], in0=inv[:, 2, 0:n], scalar=float(TPAD),
                                            in1=inv[:, 0, 0:n], op0=ALU.mult, op1=ALU.add))
                link(v.scalar_tensor_tensor(out=row_f[:, 0, 0:n], in0=inv[:, 1, 0:n], scalar=float(P),
                                            in1=row_f[:, 0, 0:n], op0=ALU.mult, op1=ALU.add))
                link(v.tensor_scalar(row_f[:, 1, 0:n], inv[:, 3, 0:n], -1.0, 1.0, ALU.mult, ALU.add))
                link(v.tensor_tensor(row_f[:, 1, 0:n], row_f[:, 1, 0:n], spare[:, m, 0:n], ALU.mult))
                v.tensor_tensor(row_id[:, 0:n], row_f[:, 0, 0:n], row_f[:, 1, 0:n], ALU.add)\
                    .then_inc(S["v_id"], 1)

                def gathered(i):
                    lo, hi = r["groups"][i]
                    dve.wait_ge(S["p_gt"], 10 * m + 2 * i + 2)
                    v.tensor_copy(xgt[:, 1, lo * P:hi * P], ps[0:DH, 7, 0:(hi - lo) * P])\
                        .then_inc(S["v_gt"], 1)

                def product(j, s):
                    dve.wait_ge(S["a_sg"], j * 2 + (s + 1 + 2 * before))
                    v.tensor_tensor(ht[:, s, 0:half], sg[:, s, 0:half], ps[:, 2 * s + 1, 0:half], ALU.mult)\
                        .then_inc(S["v_ht"], 1)

                gathered(0)
                for j in range(3):
                    product(j, 0)
                    if j == 2:
                        gathered(3)
                    product(j, 1)
                    gathered((1, 2, 4)[j])
                with dve.Fori(2, n // 2) as i:
                    for b in (1, 0):
                        product(i * 2 - b, 0)
                        product(i * 2 - b, 1)
                product(n - 1, 0)
                product(n - 1, 1)

            def routed(t):
                rows = P if t < TT - 1 else LAST
                dve.wait_ge(S["d_yg"], 32)
                v.scalar_tensor_tensor(out=h[0:rows, t, :], in0=yg[0][0:rows, 0, t, :],
                                       scalar=gate[0:rows, 0, t:t + 1], in1=h[0:rows, t, :],
                                       op0=ALU.mult, op1=ALU.add).then_inc(S["v_h"], 1)

            experts(0, attended)

            layer_norm(3, routed, h, "v_h", 2 * TT, 2 * TT + 1, dst=xn2)
            dve.wait_ge(S["a_std"], 3 * TT + 2)
            link(v.reciprocal(rstd2[:], std2[:]))
            for t in range(TT):
                v.tensor_scalar(xn[:, t, :], h[:, t, :], mv[:, t, 0:1], rstd2[:, t:t + 1],
                                ALU.subtract, ALU.mult).then_inc(S["v_xn"], 1)
            transposed(3, padded=True, ln=ln1)
            v.tensor_scalar(nega[:, 2], alog[:], 88.7, None, ALU.min).then_inc(S["v_u"], 1)
            dve.wait_ge(S["p_dt"], 2)
            link(v.tensor_tensor(dtw[:, 0], ps[:, 4, 0:PAIRS * SSH].rearrange("p (j h) -> p j h", h=SSH),
                                 dtb[:].unsqueeze(1).broadcast_to([P, PAIRS, SSH]), ALU.add))
            v.scalar_tensor_tensor(out=dtw[:, 1].rearrange("p j h -> p (j h)"),
                                   in0=dtw[:, 0].rearrange("p j h -> p (j h)"), scalar=-1.0,
                                   in1=dtw[:, 0].rearrange("p j h -> p (j h)"), op0=ALU.mult, op1=ALU.max)\
                .then_inc(S["v_u"], 1)
            dve.wait_ge(S["a_dt"], 2)
            v.tensor_scalar(dtw[:, 3], dtw[:, 2], 1.0, None, ALU.add).then_inc(S["v_one"], 1)
            dve.wait_ge(S["v_one"], 1)
            link(v.reciprocal(dtw[:, 5], dtw[:, 3]))
            link(v.tensor_scalar(dtw[:, 6], dtw[:, 3], -1.0, None, ALU.add))
            link(v.tensor_tensor(dtw[:, 6], dtw[:, 2], dtw[:, 6], ALU.subtract))
            link(v.tensor_tensor(dtw[:, 6], dtw[:, 6], dtw[:, 5], ALU.mult))
            dve.wait_ge(S["a_dt"], 3)
            link(v.tensor_tensor(dtw[:, 6], dtw[:, 6], dtw[:, 4], ALU.add))
            link(v.scalar_tensor_tensor(out=dtw[:, 7].rearrange("p j h -> p (j h)"),
                                        in0=dtw[:, 0].rearrange("p j h -> p (j h)"), scalar=0.0,
                                        in1=dtw[:, 6].rearrange("p j h -> p (j h)"), op0=ALU.max, op1=ALU.add))
            link(v.tensor_scalar(nega[:, 1], nega[:, 0], 1e30, None, ALU.min))
            link(v.tensor_tensor(dtw[:, 1], dtw[:, 7], nega[:, 1].unsqueeze(1).broadcast_to([P, PAIRS, SSH]),
                                 ALU.mult))
            link(v.tensor_scalar(dtw[:, 3], dtw[:, 7], 1.0, None, ALU.min))
            link(v.tensor_tensor(dtw[:, 3], dtw[:, 3], nega[:, 0].unsqueeze(1).broadcast_to([P, PAIRS, SSH]),
                                 ALU.mult))
            link(v.tensor_tensor(dtw[:, 1], dtw[:, 1], dtw[:, 3], ALU.max))
            v.tensor_scalar(dtw[:, 1], dtw[:, 1], 200.0, -1.0, ALU.min, ALU.mult).then_inc(S["v_la"], 1)
            for s, r in enumerate((3, 0, 1, 2)):
                dve.wait_ge(S["a_cv"], s + 1)
                for k in range(1, DC):
                    v.scalar_tensor_tensor(out=cv[:, r], in0=xpad[:, r, :, k:k + NTOK],
                                           scalar=convw[:, r, k:k + 1], in1=cv[:, r],
                                           op0=ALU.mult, op1=ALU.add).then_inc(S["v_cv"], 1)
                    dve.wait_ge(S["v_cv"], s * (DC - 1) + k)
            dve.wait_ge(S["p_g"], 1)
            v.tensor_tensor(gm[:], ps[:, 7, 0:PAIRS * NTOK].rearrange("p (j n) -> p j n", n=NTOK)
                            .unsqueeze(2).broadcast_to([P, PAIRS, 2, NTOK]),
                            causal[:].unsqueeze(1).broadcast_to([P, PAIRS, 2, NTOK]), ALU.mult)\
                .then_inc(S["v_gm"], 1)
            for j in range(PAIRS):
                dve.wait_ge(S["p_xs"], j + 1)
                v.tensor_tensor(dtx[:, j, :].rearrange("p (h d) -> p h d", d=SSD),
                                ps[:, 6 + j % 2, 0:DI].rearrange("p (h d) -> p h d", d=SSD),
                                dtw[:, 7, j, :].unsqueeze(2).broadcast_to([P, SSH, SSD]), ALU.mult)\
                    .then_inc(S["v_dtx"], 1)
                if j % 2 == 1:
                    continue
                if j == 0:
                    dve.wait_ge(S["v_gm"], 1)
                dve.wait_ge(S["a_dec"], j // 2 + 1)
                v.tensor_tensor(mix[:, j], dec[:, j].unsqueeze(2).broadcast_to([P, SSH, 2, NTOK]),
                                gm[:, j].unsqueeze(1).broadcast_to([P, SSH, 2, NTOK]), ALU.mult)\
                    .then_inc(S["v_mix"], 1)
            dve.wait_ge(S["p_ys"], 1)
            dve.wait_ge(S["g_ssm"], 4)
            dve.wait_ge(S["a_xs"], 5)
            for r in range(HP):
                for b in range(2):
                    v.scalar_tensor_tensor(
                        out=yt[:, r, HB * b:HB * b + HB].rearrange("p (i n) -> p i n", n=NTOK),
                        in0=xst[:, r, 8 * b:8 * b + 8, 0:NTOK], scalar=dskip[:, r:r + 1],
                        in1=ps[:, 2 * r + b, 0:HB].rearrange("p (i n) -> p i n", n=NTOK),
                        op0=ALU.mult, op1=ALU.add).then_inc(S["v_ys"], 1)
                dve.wait_ge(S["v_ys"], 2 * r + 2)
                dve.wait_ge(S["a_z"], r + 1)
                v.tensor_tensor(yt[:, r, 0:T], yt[:, r, 0:T], zs[:, r, :], ALU.mult).then_inc(S["v_yz"], 1)
            dve.wait_ge(S["a_std"], 3 * TT + 3)
            link(v.reciprocal(rstd2[:], std2[:]))

            def scanned(t):
                dve.wait_ge(S["p_out"], t + 1)
                v.scalar_tensor_tensor(out=x2[:, t, :], in0=ps[:, TILE_BANK[t], 0:D],
                                       scalar=rstd2[:, t:t + 1], in1=xn[:, t, :], op0=ALU.mult, op1=ALU.add)\
                    .then_inc(S["v_x2"], 1)

            layer_norm(4, scanned, x2, "v_x2", 0, 3 * TT + 3)
            transposed(4, ln=ln2)
            for r in range(HP):
                dve.wait_ge(S["a_fc"], r + 1)
                v.tensor_tensor(ft[:, r, 0:T].rearrange("p (b n) -> p b n", b=2), two_halves(4 * (r % 2)),
                                sgf[:, r, 0:T].rearrange("p (b n) -> p b n", b=2), ALU.mult)\
                    .then_inc(S["v_fc"], 1)
            dve.wait_ge(S["g_hb"], 2)

            def fed_forward(t):
                dve.wait_ge(S["p_f2"], t + 1)
                v.tensor_tensor(h[:, t, :], ps[:, TILE_BANK[t], 0:D], hb[:, t, :], ALU.add)\
                    .then_inc(S["v_h"], 1)

            experts(1, fed_forward)
            for k in range(2):
                dve.wait_ge(S[("d_yg", "d_yg2")[k]], (64, 32)[k])
                for t in range(TT):
                    rows = P if t < TT - 1 else LAST
                    if k == 1:
                        dve.wait_ge(S["v_h"], 4 * TT + t + 1)
                    v.scalar_tensor_tensor(out=h[0:rows, t, :], in0=yg[1][0:rows, k, t, :],
                                           scalar=gate[0:rows, k, t:t + 1], in1=h[0:rows, t, :],
                                           op0=ALU.mult, op1=ALU.add).then_inc(S["v_h"], 1)

        @block.tensor
        def _(pe):
            mm = nc.tensor.matmul

            def keep_busy(bank, n):
                for _ in range(n):
                    mm(ps[:, bank, :], busy[:, 0:P], busy[:], start=True, stop=True)

            pe.wait_ge(S["g_const"], N_FIRST)
            keep_busy(0, WARM_START)

            def chunk(n, t):
                return mm(ps[:, TILE_BANK[t], 0:D], xp[:, n % RING, t * P:t * P + P], weff[:, n, :],
                          start=(n == 0), stop=(n == NCH - 1))

            for n in range(NCH - 8):
                if n in (0, 4, 8):
                    pe.wait_ge(S["v_weff"], WEFF[n // 4])
                pe.wait_ge(S["a_xp"], n + 1)
                for t in range(TT):
                    ins = chunk(n, t)
                ins.then_inc(S["p_ch"], 1)
            pe.wait_ge(S["v_weff"], WEFF[-1])
            pe.wait_ge(S["a_xp"], NCH)
            for t in range(TT):
                for n in range(NCH - 8, NCH):
                    ins = chunk(n, t)
                ins.then_inc(S["p_ht"], 1)
                if t == 1:
                    pe.wait_ge(S["v_st"], SUMS + 2)
                    pe.wait_ge(S["g_sq"], SUMS + 2)
                    for u in range(TT):
                        for s in range(2):
                            ins = mm(ps[:, 2, 2 * u + s:2 * u + s + 1], tot[:, s, u * P:u * P + P], inv_k[:],
                                     start=True, stop=True)
                    ins.then_inc(S["p_st"], 1)
                    for s in range(2):
                        pe.wait_ge(S["v_acc"], 1 if s == 0 else 5)
                        mm(ps[:, 3, s * D:s * D + D], ones[:], acc[:, s, :], start=True, stop=True)\
                            .then_inc(S["p_st"], 1)

            def transposes(i, src, count):
                for t in range(TT):
                    pe.wait_ge(S["v_xn"], count + t + 1)
                    for m in range(DM):
                        ins = nc.tensor.transpose(row_of(2 * m, 2, DH)[:, t * P:t * P + P],
                                                  src[:, t, m * DH:m * DH + DH], ident[:])
                        if t == TT - 1:
                            ins.then_inc(S["p_tr"], 1)
                    keep_busy(TILE_BANK[t % 4], 2)
                pe.wait_ge(S["a_xt"], i)
                pe.wait_ge(S["v_xt"], i)

            def windows(m, b):
                return xtp[:, m, 8 * b:8 * b + 8, 0:NTOK]

            transposes(1, xn, 0)
            pe.wait_ge(S["d_att"], N_ATT)
            for r in range(4):
                if r == 2:
                    for j in range(PAIRS):
                        for m in range(DM):
                            ins = mm(ps[:, j // 2, (j % 2) * D:(j % 2 + 1) * D],
                                     xtp[:, m, 2 * j:2 * j + 2, :].rearrange("p i n -> p (i n)"),
                                     wqkv[:, m, 2 * D:3 * D], start=(m == 0), stop=(m == 1))
                    ins.then_inc(S["p_v"], 1)
                if r >= 2:
                    pe.wait_ge(S["a_qf"], r - 1)
                for m in range(DM):
                    for b in range(2):
                        ins = mm(ps[0:DH, 4 + 2 * (r % 2) + b, 0:HB], wqkv[:, m, DH * r:DH * r + DH], windows(m, b),
                                 start=(m == 0), stop=(m == 1))
                ins.then_inc(S["p_qk"], 1)

            def scores(j):
                if j == 0:
                    pe.wait_ge(S["a_vf"], 1)
                    keep_busy(0, WARM_SCORES)
                    pe.wait_ge(S["v_qe"], 2 * HH)
                    pe.wait_ge(S["v_ki"], 2)
                    pe.wait_ge(S["a_qf"], 4)
                if j >= 3:
                    pe.wait_ge(S["v_pre"], j - 2)
                for i in range(2):
                    for m in range(DM):
                        ins = mm(ps[64 * i:64 * i + 64, 4 + j % 3, m * HH * NTOK:(m + 1) * HH * NTOK],
                                 ki[:, m, 2 * j + i, :],
                                 qe[:, m, 2 * j + i].rearrange("p h n -> p (h n)"), start=True, stop=True)
                ins.then_inc(S["p_sc"], 1)

            def attend(j):
                if j == 0:
                    pe.wait_ge(S["v_vi"], 2)
                pe.wait_ge(S["a_at"], j + 1)
                for i in range(2):
                    for hh in range(HEADS):
                        ins = mm(ps[64 * i:64 * i + 64, j // 2, (j % 2) * D + hh * HD:(j % 2) * D + (hh + 1) * HD],
                                 at[:, j % 2, hh * NTOK:hh * NTOK + 64], vi[:, i, j, hh * HD:(hh + 1) * HD],
                                 start=True, stop=True)
                ins.then_inc(S["p_av"], 1)

            for j in range(PAIRS + 3):
                if j >= 3:
                    if j == 3:
                        keep_busy(7, 5)
                    attend(j - 3)
                if j < PAIRS:
                    scores(j)
            for m in range(DM):
                for j in range(PAIRS):
                    if m == 0 and j % 2 == 0:
                        keep_busy(7, 1)
                    pe.wait_ge(S["v_oi"], j // 2 + 1)
                    ins = nc.tensor.transpose(ps[0:DH, 4 + m, :].bitcast(BF16)[:, j * P:j * P + P],
                                              oi[:, j, m * DH:m * DH + DH], identb[:])
                ins.then_inc(S["p_otr"], 1)
            keep_busy(7, 3)
            pe.wait_ge(S["a_ot"], 1)
            pe.wait_ge(S["v_ot"], 1)
            for t in range(TT):
                for m in range(DM):
                    ins = mm(ps[:, TILE_BANK[t], 0:D], ot[:, m, t * P:t * P + P],
                             wproj[:, m, :], start=(m == 0), stop=(m == 1))
                ins.then_inc(S["p_proj"], 1)

            def experts(m_):
                r = MOE[m_]
                n, hid, before = r["n"], r["hid"], r["before"]
                tiles = hid // P // 2
                transposes(2 if m_ == 0 else 5, xn, TT if m_ == 0 else 5 * TT)
                for t in range(TT):
                    for m in range(DM):
                        ins = mm(ps[:, 6, t * E:t * E + E], xt[:, m, t * P:t * P + P], rw[m_][:, m, :],
                                 start=(m == 0), stop=(m == 1))
                ins.then_inc(S["p_lg"], 1)
                pe.wait_ge(S["v_oh"], m_ + 1)
                for t in range(TT):
                    for u in range(t):
                        mm(ps[:, 7, t * E:t * E + E], onesb[:], ohb[:, u, :], start=(u == 0), stop=False)
                    mm(ps[:, 7, t * E:t * E + E], earlier[:], ohb[:, t, :], start=(t == 0), stop=True)
                for t in range(TT):
                    k = P if t < TT - 1 else LAST
                    ins = mm(ps[:, 7, TT * E:TT * E + E], onesb[0:k, :], ohb[0:k, t, :], start=(t == 0),
                             stop=(t == TT - 1))
                ins.then_inc(S["p_rk"], 1)
                pe.wait_ge(S["v_inv"], m_ + 1)
                for i in range(r["k"] * TT):
                    k = P if i % TT < TT - 1 else LAST
                    ins = mm(ps[:, 5, 0:4 * n], at_r[0:k, i, :],
                             val_n[0:k, i, :, 0:n], start=(i == 0), stop=(i == r["k"] * TT - 1))
                ins.then_inc(S["p_inv"], 1)

                def gathered(i):
                    lo, hi = r["groups"][i]
                    lo1, hi1 = MOE[0]["groups"][i]
                    pe.wait_ge(S[f"d_xg{i}"], 16 * (hi - lo + m_ * (hi1 - lo1)))
                    if i >= 1:
                        pe.wait_ge(S["a_gt"], 5 * m_ + i)
                        pe.wait_ge(S["v_gt"], 5 * m_ + i)
                    for m in range(DM):
                        for c in range(hi - lo):
                            ins = nc.tensor.transpose(ps[0:DH, 6 + m, c * P:c * P + P],
                                                      xg[:, lo + c, m * DH:m * DH + DH], ident[:])
                        ins.then_inc(S["p_gt"], 1)

                pe.wait_ge(S["v_src"], m_ + 1)
                keep_busy(0, WARM_SORTED[m_])
                gathered(0)
                pe.wait_ge(S["a_gt"], 5 * m_ + 1)
                pe.wait_ge(S["v_gt"], 5 * m_ + 1)

                def up(j, b, s, wait=True):
                    if s == 0:
                        pe.wait_ge(d_w12[b], (j + (2 - b)) * 8 + 8 * before)
                    if wait:
                        pe.wait_ge(S["v_ht"], j * 2 + (s - 1 + 2 * before))
                    for g in range(2):
                        for c in range(tiles):
                            col = g * hid + (s * tiles + c) * P
                            for m in range(DM):
                                ins = mm(ps[:, 2 * s + g, c * P:c * P + P], w12[b][:, m, col:col + P],
                                         xgt[:, m, bass.ds(j * P, P)], start=(m == 0), stop=(m == 1))
                    ins.then_inc(S["p_gu"], 1)

                def down(j, b, s, wait=True):
                    pe.wait_ge(S["v_ht"], j * 2 + (s + 1 + 2 * before))
                    if s == 0:
                        pe.wait_ge(d_w3[b], (j + (2 - b)) * 8 + 8 * before)
                    if s == 0 and wait:
                        pe.wait_ge(S["a_y"], j + (before - 1))
                    for c in range(tiles):
                        ins = mm(ps[:, 4 + b, 0:D], ht[:, s, c * P:c * P + P], w3[b][:, s * tiles + c, :],
                                 start=(s == 0 and c == 0), stop=(s == 1 and c == tiles - 1))
                    if s == 1:
                        ins.then_inc(S["p_y"], 1)

                up(0, 0, 0, wait=False)
                up(0, 0, 1, wait=False)
                gathered(1)
                down(0, 0, 0, wait=False)
                for j in (1, 2):
                    if j == 1:
                        pe.wait_ge(S["a_gt"], 5 * m_ + 2)
                        pe.wait_ge(S["v_gt"], 5 * m_ + 2)
                    up(j, j % 2, 0)
                    if j == 2:
                        gathered(3)
                    down(j - 1, 1 - j % 2, 1)
                    up(j, j % 2, 1)
                    gathered(2 * j)
                    down(j, j % 2, 0, wait=(j == 2))
                pe.wait_ge(S["a_gt"], 5 * m_ + 5)
                pe.wait_ge(S["v_gt"], 5 * m_ + 5)
                with pe.Fori(2, n // 2) as i:
                    for b in (1, 0):
                        j = i * 2 - b
                        up(j, b, 0)
                        down(j - 1, 1 - b, 1)
                        up(j, b, 1)
                        down(j, b, 0)
                up(n - 1, 1, 0)
                down(n - 2, 0, 1)
                up(n - 1, 1, 1)
                down(n - 1, 1, 0)
                down(n - 1, 1, 1)

            experts(0)

            pe.wait_ge(S["v_h"], 2 * TT + 1)
            keep_busy(0, WARM_NORM)
            transposes(3, xn2, 2 * TT)
            for m in range(DM):
                for b in range(2):
                    ins = mm(ps[0:SSH, 6 + b, 0:HB], inproj[:, m, 2 * DI + 2 * SSN:], windows(m, b),
                             start=(m == 0), stop=(m == 1))
            ins.then_inc(S["p_dt"], 1)
            cols = (2 * DI, DI, DI + P, DI + 2 * P, 0, P, 2 * P)
            for s, c0 in enumerate(cols):
                if s == 1:
                    pe.wait_ge(S["a_dtr"], 1)
                    for j in range(PAIRS):
                        ins = nc.tensor.transpose(ps[:, 4, j * SSH:j * SSH + SSH],
                                                  dtr[:, 2 * j:2 * j + 2, :].rearrange("p i n -> p (i n)"),
                                                  ident[0:SSH, 0:SSH])
                    ins.then_inc(S["p_dt"], 1)
                if s == 2:
                    pe.wait_ge(S["v_u"], 2)
                if s >= 4:
                    pe.wait_ge(S["a_cp"], 2 * (s - 3))
                for m in range(DM):
                    for b in range(2):
                        ins = mm(ps[:, 2 * (s % 4) + b, 0:HB], inproj[:, m, c0:c0 + P], windows(m, b),
                                 start=(m == 0), stop=(m == 1))
                ins.then_inc(S["p_in"], 1)
            pe.wait_ge(S["g_av"], 1)
            pe.wait_ge(S["a_z"], 2)
            for j in range(PAIRS):
                ins = mm(ps[:, j // 2, (j % 2) * SEGW:(j % 2 + 1) * SEGW], later_blk[:],
                         av[:, j].rearrange("p h n -> p (h n)"), start=True, stop=True)
                if j % 2 == 1:
                    ins.then_inc(S["p_seg"], 1)
            pe.wait_ge(S["a_cp"], 8)
            pe.wait_ge(S["a_xs"], 2)
            for b in range(IMGS):
                i = b % 2
                ins = mm(ps[64 * i:64 * i + 64, 7, (b // 2) * NTOK:(b // 2 + 1) * NTOK], bt[:, b, :],
                         ct[:, b, 0:NTOK], start=True, stop=True)
            ins.then_inc(S["p_g"], 1)
            pe.wait_ge(S["a_xs"], 5)

            def token_major(j):
                if j == 1:
                    pe.wait_ge(S["v_gm"], 1)
                if j >= 2:
                    pe.wait_ge(S["v_dtx"], j - 1)
                for r in range(HP):
                    ins = nc.tensor.transpose(ps[:, 6 + j % 2, r * P:r * P + P],
                                              xst[:, r, 2 * j:2 * j + 2, :].rearrange("p i n -> p (i n)"),
                                              ident[:])
                ins.then_inc(S["p_xs"], 1)

            def scan(j):
                if j == 0:
                    pe.wait_ge(S["a_dec"], 4)
                    pe.wait_ge(S["a_z"], 3)
                pe.wait_ge(S["v_dtx"], j + 1)
                pe.wait_ge(S["v_mix" if j % 2 == 0 else "g_mix"], j // 2 + 1)
                for hh in range(SSH):
                    o = 64 * (hh % 2)
                    ins = mm(ps[o:o + 64, 2 * (hh // 2) + j // 4, (j % 4) * 2 * NTOK:(j % 4 + 1) * 2 * NTOK],
                             dtx[:, j, hh * SSD:(hh + 1) * SSD], mix[:, j, hh].rearrange("p i n -> p (i n)"),
                             start=True, stop=True)
                if j == PAIRS - 1:
                    ins.then_inc(S["p_ys"], 1)

            for j in range(PAIRS + 2):
                if j < PAIRS:
                    token_major(j)
                if j >= 2:
                    scan(j - 2)
            keep_busy(6, 6)
            for r in range(HP):
                pe.wait_ge(S["a_ysq"], r + 1)
                for b in range(2):
                    ins = mm(ps[0:1, 6 + b, 0:HB], ones[:, 0:1], ysq[:, r, HB * b:HB * b + HB],
                             start=(r == 0), stop=(r == HP - 1))
            ins.then_inc(S["p_ssq"], 1)
            pe.wait_ge(S["v_yz"], HP)
            pe.wait_ge(S["g_ssm"], 4)
            pe.wait_ge(S["g_wout"], 1)
            for t in range(TT):
                if t == 1:
                    pe.wait_ge(S["a_ssr"], 1)
                    pe.wait_ge(S["g_ssm"], 6)
                    for u in range(TT):
                        ins = nc.tensor.transpose(ps[:, 3, u:u + 1], ssr[:, u * P:u * P + P], ident[0:1, 0:1])
                    ins.then_inc(S["p_ssq"], 1)
                for r in range(HP):
                    ins = mm(ps[:, TILE_BANK[t], 0:D], yt[:, r, t * P:t * P + P], outproj[:, r, :],
                             start=(r == 0), stop=(r == HP - 1))
                ins.then_inc(S["p_out"], 1)
            pe.wait_ge(S["a_std"], 3 * TT + 3)
            transposes(4, xn, 4 * TT)
            for r in range(HP):
                if r == 2:
                    pe.wait_ge(S["v_fc"], 1)
                for g in range(2):
                    for m in range(DM):
                        for b in range(2):
                            ins = mm(ps[:, 4 * (r % 2) + 2 * g + b, 0:HB],
                                     fc1[:, m, g * DI + r * P:g * DI + r * P + P],
                                     xt[:, m, HB * b:HB * b + HB], start=(m == 0), stop=(m == 1))
                    ins.then_inc(S["p_fc"], 1)
            pe.wait_ge(S["v_fc"], HP)
            for t in range(TT):
                for r in range(HP):
                    ins = mm(ps[:, TILE_BANK[t], 0:D], ft[:, r, t * P:t * P + P],
                             fc2[:, r, :], start=(r == 0), stop=(r == HP - 1))
                ins.then_inc(S["p_f2"], 1)
            experts(1)


def _halves(w):
    return w.reshape(DM, DH, -1).transpose(1, 0, 2)


def _chunks(w):
    return w.reshape(-1, P, w.shape[-1]).transpose(1, 0, 2)


def _patch_rows(w):
    n = w.shape[0]
    w = w.reshape(n, 2, 8, 2, 8, 5, CH)
    sh = np.stack([w[..., s, :] for s in (1, 3, 4, 2)])
    sh = sh.transpose(4, 3, 5, 6, 2, 0, 1)
    sh = sh.reshape(P, NCH, n)
    un = w[..., 0, :]
    un = un[:, ::-1, :, ::-1]
    un = un.transpose(3, 2, 4, 5, 1, 0).reshape(P, CH * 2, n)
    return sh, un


def _rows(w):
    return np.broadcast_to(w.reshape(1, -1), (P, w.size))


def kernel(**inputs):
    import concourse.bacc as bacc
    from concourse.bass_utils import run_bass_kernel_spmd

    x = {k: np.asarray(v) for k, v in inputs.items()}
    a = {}
    img = np.pad(x["x"], ((0, 0), (0, 0), (8, 8), (8, 8))).reshape(IMGS, CH, WIN, 2, 8, WIN, 2, 8)
    a["xw"] = img.transpose(6, 4, 7, 1, 3, 0, 2, 5).reshape(P, CH, 2, NWIN)
    a["w_sh"], a["w_un"] = _patch_rows(x["L0_tok_W"])
    for name, src in (("gam", "L0_tok_ln_gamma"), ("bet", "L0_tok_ln_beta")):
        sh, un = _patch_rows(x[src].reshape(1, -1))
        a[name] = np.concatenate([sh, un], axis=1)[:, :, 0]
    a["tok_b"] = x["L0_tok_b"].reshape(1, D)
    a["wqkv"] = _halves(x["L0_attn_Wqkv"].T)
    a["wproj"] = _halves(x["L0_attn_Wproj"].T)
    a["bproj"] = _rows(x["L0_attn_bproj"])
    a["scales"] = _rows(np.stack([x["L0_attn_s_" + s].reshape(()) for s in ("q", "k", "v", "attn", "after")]))
    a["rw1"] = _halves(x["L0_ffn_router_w"])
    a["rb1"] = _rows(x["L0_ffn_router_b"])
    a["rw2"] = _halves(x["L1_ffn_router_w"].T)
    a["m1_w12"] = np.concatenate([x["L0_ffn_w1"], x["L0_ffn_w2"]], axis=2)\
        .reshape(E, DM, DH, 2 * M1_H).transpose(0, 2, 1, 3)
    a["m1_w3"] = x["L0_ffn_w3"].reshape(E, M1_H // P, P, D).transpose(0, 2, 1, 3)
    a["m2_w12"] = np.concatenate([x["L1_ffn_Wg"], x["L1_ffn_Wu"]], axis=1).transpose(0, 2, 1)\
        .reshape(E, DM, DH, 2 * M2_H).transpose(0, 2, 1, 3)
    a["m2_w3"] = x["L1_ffn_Wd"].transpose(0, 2, 1).reshape(E, M2_H // P, P, D).transpose(0, 2, 1, 3)
    L = "L1_attn_"
    a["inproj"] = _halves(x[L + "in_proj_w"].T)
    a["convw"] = _chunks(x[L + "conv_w"])
    a["convb"] = x[L + "conv_b"].reshape(HP + 1, P).T
    a["dskip"] = np.repeat(x[L + "D_skip"], SSD).reshape(HP, P).T
    a["dtb"] = _rows(x[L + "dt_bias"])
    a["alog"] = _rows(x[L + "A_log"])
    a["normw"] = x[L + "ssm_norm_w"].reshape(HP, P).T
    a["outproj"] = _chunks(x[L + "out_proj_w"].T)
    a["fc1"] = _halves(x[L + "fc1_w"].T)
    a["fc2"] = _chunks(x[L + "fc2_w"].T)
    for i in (1, 2):
        a[f"ln{i}"] = np.stack([x[L + f"ln{i}_w"].reshape(DM, DH).T, x[L + f"ln{i}_b"].reshape(DM, DH).T], axis=1)

    nc = bacc.Bacc("TRN2", target_bir_lowering=False, num_devices=1)
    arrays, aps = {}, {}
    for name, arr in a.items():
        arrays["in_" + name] = np.ascontiguousarray(arr)
        aps[name] = nc.dram_tensor("in_" + name, arr.shape, mybir.dt.from_np(arr.dtype),
                                   kind="ExternalInput").ap()
    out = nc.dram_tensor("out_h", (T, D), F32, kind="ExternalOutput").ap()
    build(nc, aps, out)
    r = run_bass_kernel_spmd(nc, [arrays], core_ids=[0])
    return r.results[0]["out_h"].reshape(IMGS, NTOK, D)
```
